# Optimizing a Trainium2 kernel written in Bass

```python
import numpy as np
import jax
import jax.numpy as jnp

def _softmax(x, axis=-1):
    return jax.nn.softmax(x, axis=axis)

def _gelu(x):
    return jax.nn.gelu(x, approximate=True)

def _silu(x):
    return jax.nn.silu(x)

def _sigmoid(x):
    return jax.nn.sigmoid(x)

def _layernorm(x, axis=-1, eps=1e-05):
    m = jnp.mean(x, axis=axis, keepdims=True)
    v = jnp.var(x, axis=axis, keepdims=True)
    return (x - m) / jnp.sqrt(v + eps)

def _scatter_add(tgt, idx, src, axis=0):
    return tgt.at[idx].add(src)

def _segment_sum(src, seg, n):
    return jax.ops.segment_sum(src, seg, n)
kernel_name = 'mk_macaron_d1_jaxref_r4_c5503c'

def setup_inputs(seed: int=0):
    np.random.seed(seed)
    _w = jnp.asarray

    def _L0_attn_setup():
        import jax, jax.numpy as jnp
        import numpy as np
        from jax import lax
        BLOCK_LEN = 128
        NEG_INF = -1000000000.0
        key = jax.random.key(seed)
        ks = jax.random.split(key, 8)
        N, L, Dm = (2, 2048, 1024)
        W, H, dh = (256, 16, 64)
        s = lambda fan: 1.0 / np.sqrt(fan)
        return {'inputs': jax.random.normal(ks[0], (N, L, Dm), jnp.float32), 'conv_w': jax.random.normal(ks[1], (3, Dm, 3 * W), jnp.float32) * s(3 * Dm), 'conv_b': jnp.zeros((3 * W,), jnp.float32), 'wq': jax.random.normal(ks[2], (W, H, dh), jnp.float32) * s(W), 'bq': jnp.zeros((H, dh), jnp.float32), 'wk': jax.random.normal(ks[3], (W, H, dh), jnp.float32) * s(W), 'bk': jnp.zeros((H, dh), jnp.float32), 'wv': jax.random.normal(ks[4], (W, H, dh), jnp.float32) * s(W), 'bv': jnp.zeros((H, dh), jnp.float32), 'wo': jax.random.normal(ks[5], (H, dh, W), jnp.float32) * s(H * dh), 'bo': jnp.zeros((W,), jnp.float32), 'proj_w': jax.random.normal(ks[6], (W, Dm), jnp.float32) * s(W), 'proj_b': jnp.zeros((Dm,), jnp.float32)}
    _L0_attn_in = _L0_attn_setup()

    def _L0_ffn_setup():
        import jax, jax.numpy as jnp
        import numpy as np

        @jax.custom_vjp
        def ste_sign(w):
            return jnp.sign(w)

        def _ste_fwd(w):
            return (jnp.sign(w), w)

        def _ste_bwd(w, g):
            mask = ((w > -1) & (w < 1)).astype(g.dtype)
            return (g * mask,)
        ste_sign.defvjp(_ste_fwd, _ste_bwd)
        key = jax.random.key(seed)
        k = jax.random.split(key, 6)
        B, S, H, O, E = (4, 512, 1024, 1024, 8)
        return {'x': jax.random.normal(k[0], (B, S, H), dtype=jnp.float32), 'weight': jax.random.normal(k[1], (O, H), dtype=jnp.float32) * 0.02, 'bias': jax.random.normal(k[2], (O,), dtype=jnp.float32) * 0.02, 'gate_w': jax.random.normal(k[3], (E, H), dtype=jnp.float32) * 0.02, 'in_channel_scale': jax.random.normal(k[4], (E, H), dtype=jnp.float32), 'out_channel_scale': jax.random.normal(k[5], (E, O), dtype=jnp.float32)}
    _L0_ffn_in = _L0_ffn_setup()
    _d = {'L0_attn_inputs': _L0_attn_in['inputs'], 'L0_attn_conv_w': _L0_attn_in['conv_w'], 'L0_attn_conv_b': _L0_attn_in['conv_b'], 'L0_attn_wq': _L0_attn_in['wq'], 'L0_attn_bq': _L0_attn_in['bq'], 'L0_attn_wk': _L0_attn_in['wk'], 'L0_attn_bk': _L0_attn_in['bk'], 'L0_attn_wv': _L0_attn_in['wv'], 'L0_attn_bv': _L0_attn_in['bv'], 'L0_attn_wo': _L0_attn_in['wo'], 'L0_attn_bo': _L0_attn_in['bo'], 'L0_attn_proj_w': _L0_attn_in['proj_w'], 'L0_attn_proj_b': _L0_attn_in['proj_b'], 'L0_ffn_weight': _L0_ffn_in['weight'], 'L0_ffn_bias': _L0_ffn_in['bias'], 'L0_ffn_gate_w': _L0_ffn_in['gate_w'], 'L0_ffn_in_channel_scale': _L0_ffn_in['in_channel_scale'], 'L0_ffn_out_channel_scale': _L0_ffn_in['out_channel_scale']}
    _x0 = _d['L0_attn_inputs']
    _d['L0_attn_inputs'] = jax.random.normal(jax.random.fold_in(jax.random.key(seed), 1), (1, 2048, 1024), dtype=_x0.dtype)
    del _x0
    return _d

def reference(L0_attn_inputs, L0_attn_conv_w, L0_attn_conv_b, L0_attn_wq, L0_attn_bq, L0_attn_wk, L0_attn_bk, L0_attn_wv, L0_attn_bv, L0_attn_wo, L0_attn_bo, L0_attn_proj_w, L0_attn_proj_b, L0_ffn_weight, L0_ffn_bias, L0_ffn_gate_w, L0_ffn_in_channel_scale, L0_ffn_out_channel_scale):

    def _L0_attn_ref(inputs, conv_w, conv_b, wq, bq, wk, bk, wv, bv, wo, bo, proj_w, proj_b):
        import jax, jax.numpy as jnp
        import numpy as np
        from jax import lax
        BLOCK_LEN = 128
        NEG_INF = -1000000000.0
        N, L, Dm = inputs.shape
        x = lax.conv_general_dilated(inputs, conv_w, window_strides=(1,), padding='SAME', dimension_numbers=('NWC', 'WIO', 'NWC')) + conv_b
        q, k, v = jnp.split(x, 3, axis=-1)
        W_ = q.shape[-1]
        nb = L // BLOCK_LEN
        q = q.reshape(N * nb, BLOCK_LEN, W_)
        k = k.reshape(N * nb, BLOCK_LEN, W_)
        v = v.reshape(N * nb, BLOCK_LEN, W_)
        dh = wq.shape[-1]
        qh = jnp.einsum('btd,dhe->bthe', q, wq) + bq
        kh = jnp.einsum('btd,dhe->bthe', k, wk) + bk
        vh = jnp.einsum('btd,dhe->bthe', v, wv) + bv
        scale = 1.0 / jnp.sqrt(jnp.asarray(dh, qh.dtype))
        scores = jnp.einsum('bqhe,bkhe->bhqk', qh * scale, kh)
        causal = jnp.tril(jnp.ones((BLOCK_LEN, BLOCK_LEN), bool))
        scores = jnp.where(causal, scores, NEG_INF)
        p = jax.nn.softmax(scores, axis=-1)
        o = jnp.einsum('bhqk,bkhe->bqhe', p, vh)
        o = jnp.einsum('bqhe,hed->bqd', o, wo) + bo
        o = o.reshape(N, L, W_)
        return o @ proj_w + proj_b

    def _L0_ffn_ref(x, weight, bias, gate_w, in_channel_scale, out_channel_scale):
        import jax, jax.numpy as jnp
        import numpy as np

        @jax.custom_vjp
        def ste_sign(w):
            return jnp.sign(w)

        def _ste_fwd(w):
            return (jnp.sign(w), w)

        def _ste_bwd(w, g):
            mask = ((w > -1) & (w < 1)).astype(g.dtype)
            return (g * mask,)
        ste_sign.defvjp(_ste_fwd, _ste_bwd)
        B, S, H = x.shape
        xf = x.reshape(-1, H)
        router_logits = xf @ gate_w.T
        routing = jax.nn.softmax(router_logits.astype(jnp.float32), axis=1).astype(x.dtype)
        in_scale = routing @ in_channel_scale
        out_scale = routing @ out_channel_scale
        wb = ste_sign(weight)
        out = xf * in_scale @ wb.T * out_scale + bias
        return out.reshape(B, S, -1)
    x = L0_attn_inputs
    x = x + 0.5 * _L0_ffn_ref(_layernorm(x, axis=-1), L0_ffn_weight, L0_ffn_bias, L0_ffn_gate_w, L0_ffn_in_channel_scale, L0_ffn_out_channel_scale)
    x = x + _L0_attn_ref(_layernorm(x, axis=-1), L0_attn_conv_w, L0_attn_conv_b, L0_attn_wq, L0_attn_bq, L0_attn_wk, L0_attn_bk, L0_attn_wv, L0_attn_bv, L0_attn_wo, L0_attn_bo, L0_attn_proj_w, L0_attn_proj_b)
    x = x + 0.5 * _L0_ffn_ref(_layernorm(x, axis=-1), L0_ffn_weight, L0_ffn_bias, L0_ffn_gate_w, L0_ffn_in_channel_scale, L0_ffn_out_channel_scale)
    return x

_drawn_inputs = setup_inputs


def setup_inputs(seed=0):
    import zlib

    import numpy as np

    out = dict(_drawn_inputs(seed))
    spreads = {'L0_attn_conv_b': (0.0, 0.1),
     'L0_attn_bq': (0.0, 0.8),
     'L0_attn_bk': (0.0, 0.8),
     'L0_attn_bv': (0.0, 0.1),
     'L0_attn_bo': (0.0, 0.1),
     'L0_attn_proj_b': (0.0, 0.1)}
    factors = {'L0_ffn_bias': 8.0}
    for name, (base, spread) in spreads.items():
        noise = np.random.default_rng([zlib.crc32(name.encode()), seed]).standard_normal(out[name].shape)
        drawn = base * np.exp(spread * noise) if base else spread * noise
        out[name] = jnp.asarray(drawn.astype(out[name].dtype))
    for name, factor in factors.items():
        out[name] = (out[name] * factor).astype(out[name].dtype)
    return out
```

```python
from contextlib import ExitStack

import concourse.bass as bass
from concourse import mybir

F32 = mybir.dt.float32
F32R = mybir.dt.float32r
ALU = mybir.AluOpType
ACT = mybir.ActivationFunctionType
AX = mybir.AxisListType

P = 128
T = 2048
D = 1024
KD = D // P
E = 8
W = 256
WC = W // P
NCH = 3 * WC
TAPS = 3
H = 16
DH = 64
HE = H * DH
KH = HE // P
EPS = 1e-5
MASKED = -8e9
SCALE = 0.125
HALF = 512
FTOK = 256
FT = FTOK // P
NG = T // FTOK
PIECES = [[], [0], [1], [2, 3]]


def wait(eng, sem, value):
    if not isinstance(value, int) or value > 0:
        eng.wait_ge(sem, value)


def group_loop(eng, body):
    body(0, 0)
    with eng.Fori(0, (NG - 4) // 2) as i:
        body(2 * i + 1, 1)
        body(2 * i + 2, 0)
    for g in range(NG - 3, NG):
        body(g, g % 2)


def exists(g):
    return not isinstance(g, int) or 0 <= g < NG


def ffn_phase(nc, sems, tag, src, dst, w_t, bias, gate_t, ics, ocs, ident, X):
    def sem(name):
        return sems.enter_context(nc.semaphore(f"{tag}_{name}"))

    x_loaded = [sem(f"x_loaded{p}") for p in range(2)]
    w_loaded = [sem(f"w_loaded{s}") for s in range(4)]
    gate_loaded, bias_loaded = sem("gate_loaded"), sem("bias_loaded")
    scales_zeroed, scales_loaded = sem("scales_zeroed"), sem("scales_loaded")
    scales_split = sem("scales_split")
    w_signed = sem("w_signed")
    consts = sem("consts")
    bias_halved = sem("bias_halved")
    ln_stats, ln_mean, ln_var, ln_rstd, x_normed = (sem(n) for n in ("ln_stats", "ln_mean", "ln_var", "ln_rstd", "x_normed"))
    t_full, t_copied = sem("t_full"), sem("t_copied")
    l_full, l_copied, lt_full = sem("l_full"), sem("l_copied"), sem("lt_full")
    sm_step, sm_exp, routing_ready = sem("sm_step"), sem("sm_exp"), sem("routing_ready")
    r_full, r_copied = sem("r_full"), sem("r_copied")
    s_full, scaled, hi_done, lo_done = sem("s_full"), sem("scaled"), sem("hi_done"), sem("lo_done")
    o_full, o_copied = sem("o_full"), sem("o_copied")
    m_full, m_scaled = sem("m_full"), sem("m_scaled")
    res_loaded = [sem(f"res_loaded{t}") for t in range(FT)]
    res_biased, y_done = sem("res_biased"), sem("y_done")
    y_stored = [sem(f"y_stored{p}") for p in range(2)]
    if X is not None:
        n_stats, n_mean, n_var, n_rstd, y_normed = (sem(n) for n in ("n_stats", "n_mean", "n_var", "n_rstd", "y_normed"))
        n_full, n_copied = sem("n_full"), sem("n_copied")

    srcv = src.rearrange("(g t p) d -> g p t d", p=P, t=FT)
    dstv = dst.rearrange("(g t p) d -> g p t d", p=P, t=FT)
    wv = w_t.rearrange("(k p) o -> k p o", p=P)

    with ExitStack() as ctx:
        def sb(name, shape, dt=F32):
            return ctx.enter_context(nc.sbuf_tensor(f"{tag}_{name}", shape, dt))

        def ps(name, shape):
            return ctx.enter_context(nc.psum_tensor(f"{tag}_{name}", shape, F32))

        wsign = sb("wsign", [P, KD, D], F32R)
        a_hi = sb("a_hi", [P, 2, KD, FTOK], F32R)
        a_lo = sb("a_lo", [P, 2, KD, FTOK], F32R)
        a_f = sb("a_f", [P, 2, FTOK])
        xT = sb("xT", [P, 2, KD, FTOK])
        xin = sb("xin", [P, 2, FT, D])
        y = sb("y", [P, 2, FT, D])
        res = sb("res", [P, FT, D])
        oscale = sb("oscale", [P, 2, HALF])
        ics3 = sb("ics3", [P, D], F32R)
        ocs3 = sb("ocs3", [P, D], F32R)
        hbias = sb("hbias", [P, D])
        gateT = sb("gateT", [P, KD, E])
        logT = sb("logT", [E, FTOK])
        rt4 = sb("rt4", [P, FT, P])
        rT = sb("rT", [P, 2, FTOK], F32R)
        r_max = sb("r_max", [P, FT])
        r_exp = sb("r_exp", [P, FT, E])
        r_sum = sb("r_sum", [P, FT])
        r_hi = sb("r_hi", [P, FT, E], F32R)
        st6 = sb("st6", [P, FT, 2, 6])
        mv = sb("mv", [P, FT, 2])
        vpe = sb("vpe", [P, FT])
        rstd = sb("rstd", [P, FT])
        minus_half = sb("minus_half", [P, FT])
        nst6 = sb("nst6", [P, FT, 2, 6])
        nmv = sb("nmv", [P, FT, 2])
        nvpe = sb("nvpe", [P, FT])
        nrstd = sb("nrstd", [P, FT])
        wait_cell = sb("wait_cell", [P, 1])
        scale_rows = res
        w_raw = y

        p_t = ps("p_t", [P, HALF])
        p_n = ps("p_n", [P, HALF])
        p_r = ps("p_r", [P, HALF])
        p_o = ps("p_o", [P, HALF])
        p_s = ps("p_s", [P, 2, HALF])
        p_m = ps("p_m", [P, 2, HALF])

        with nc.Block() as block:

            @block.sync
            def _(sp):
                def load_x(g, p):
                    sp.dma_start(xin[:, p], srcv[g]).then_inc(x_loaded[p], 16)

                def load_w(k):
                    sp.dma_start(w_raw[:, (k % 4) // 2, k % 2, :], wv[k]).then_inc(w_loaded[k % 4], 16)

                def load_res(g, t):
                    sp.dma_start(res[:, t, :], srcv[g][:, t, :]).then_inc(res_loaded[t], 16)

                load_x(0, 0)
                load_x(1, 1)
                sp.dma_start(gateT[:], gate_t.rearrange("(k p) e -> p k e", p=P)).then_inc(gate_loaded, 16)
                for k in range(4):
                    load_w(k)
                sp.wait_ge(scales_zeroed, 1)
                for q in range(4):
                    sp.dma_start(scale_rows[32 * q:32 * q + E, 0, :], ics).then_inc(scales_loaded, 16)
                    sp.dma_start(scale_rows[32 * q:32 * q + E, 1, :], ocs).then_inc(scales_loaded, 16)
                sp.dma_start(hbias[:], bias.partition_broadcast(P)).then_inc(bias_loaded, 16)
                sp.wait_ge(t_full, 4)
                load_x(2, 0)
                for k in range(4, KD):
                    sp.wait_ge(w_signed, k - 3)
                    load_w(k)
                sp.wait_ge(scales_split, 2)
                for t in range(FT):
                    load_res(0, t)

                def store(g, p):
                    sp.wait_ge(y_done, 4 * g + 4)
                    sp.dma_start(dstv[g], y[:, p]).then_inc(y_stored[p], 16)

                def body(g, p):
                    if exists(g + 3):
                        sp.wait_ge(t_full, 4 * g + 8)
                        load_x(g + 3, 1 - p)
                    if exists(g - 1):
                        for t in range(FT):
                            sp.wait_ge(y_done, 4 * g - 2 + 2 * t)
                            load_res(g, t)
                        store(g - 1, 1 - p)

                group_loop(sp, body)
                store(NG - 1, (NG - 1) % 2)
                sp.wait_ge(y_stored[0], 16 * (NG // 2))
                sp.wait_ge(y_stored[1], 16 * (NG // 2))

            @block.gpsimd
            def _(pool):
                pool.memset(scale_rows[:], 0.0).then_inc(scales_zeroed, 1)
                pool.memset(minus_half[:], -0.5).then_inc(consts, 1)
                pool.memset(rt4[:], 0.0).then_inc(consts, 1)
                if X is not None:
                    pool.memset(X[:, :, 0:1], 0.0).then_inc(consts, 1)
                    pool.memset(X[:, :, T + 1:T + 2], 0.0).then_inc(consts, 1)
                def power(g):
                    wait(pool, x_normed, g)
                    pool.wait_ge(ln_var, g + 1)
                    pool.tensor_tensor(rstd[:], vpe[:], minus_half[:], ALU.pow).then_inc(ln_rstd, 1)

                pool.wait_ge(consts, 2)
                power(0)
                power(1)
                pool.wait_ge(bias_loaded, 16)
                pool.tensor_scalar(hbias[:], hbias[:], 0.5, None, ALU.mult).then_inc(bias_halved, 1)
                power(2)
                pool.wait_ge(bias_halved, 1)

                def body(g, p):
                    if exists(g + 3):
                        power(g + 3)
                    if X is not None and exists(g - 1):
                        pool.wait_ge(n_var, g)
                        pool.tensor_tensor(nrstd[:], nvpe[:], minus_half[:], ALU.pow).then_inc(n_rstd, 1)
                    for q in range(4):
                        t, h = q // 2, slice(q % 2 * HALF, q % 2 * HALF + HALF)
                        pool.wait_ge(res_loaded[t], 16 * g + 16)
                        pool.tensor_tensor(res[:, t, h], res[:, t, h], hbias[:, h], ALU.add).then_inc(res_biased, 1)
                        pool.wait_ge(res_biased, 4 * g + q + 1)
                        pool.wait_ge(m_scaled, 4 * g + q + 1)
                        pool.tensor_tensor(y[:, p, t, h], y[:, p, t, h], res[:, t, h], ALU.add).then_inc(y_done, 1)

                group_loop(pool, body)
                if X is not None:
                    pool.wait_ge(n_var, NG)
                    pool.tensor_tensor(nrstd[:], nvpe[:], minus_half[:], ALU.pow).then_inc(n_rstd, 1)

            @block.vector
            def _(dve):
                def stats(g, p):
                    wait(dve, x_normed, g)
                    dve.wait_ge(x_loaded[p], 8 * (g - p) + 16)
                    for t in range(FT):
                        for h in range(2):
                            last = dve.bn_stats(st6[:, t, h, :], xin[:, p, t, h * HALF:h * HALF + HALF])
                    last.then_inc(ln_stats, 1)
                    dve.wait_ge(ln_stats, g + 1)
                    dve.memset(wait_cell[:], 0.0)
                    for t in range(FT):
                        last = dve.bn_aggr(mv[:, t, :], st6[:, t])
                    last.then_inc(ln_mean, 1)
                    dve.wait_ge(ln_mean, g + 1)
                    wait(dve, ln_rstd, g)
                    dve.tensor_scalar(vpe[:], mv[:, :, 1], EPS, None, ALU.add).then_inc(ln_var, 1)

                def normalise(g, p):
                    dve.wait_ge(ln_rstd, g + 1)
                    for t in range(FT):
                        last = dve.tensor_scalar(xin[:, p, t, :], xin[:, p, t, :], mv[:, t, 0:1], rstd[:, t:t + 1],
                                                 ALU.subtract, ALU.mult)
                    last.then_inc(x_normed, 1)

                def softmax(g):
                    log = p_r[:, 0:FT * E].rearrange("p (t e) -> p t e", t=FT)
                    dve.wait_ge(lt_full, g + 1)
                    wait(dve, r_full, g)
                    dve.tensor_reduce(r_max[:], log, AX.X, ALU.max).then_inc(sm_step, 1)
                    dve.wait_ge(sm_step, 6 * g + 1)
                    dve.tensor_tensor(r_exp[:], log, r_max[:].unsqueeze(2).broadcast_to([P, FT, E]),
                                      ALU.subtract).then_inc(sm_step, 1)
                    dve.wait_ge(sm_exp, g + 1)
                    dve.tensor_reduce(r_sum[:], r_exp[:], AX.X, ALU.add).then_inc(sm_step, 1)
                    dve.wait_ge(sm_step, 6 * g + 3)
                    dve.reciprocal(r_max[:], r_sum[:]).then_inc(sm_step, 1)
                    dve.wait_ge(sm_step, 6 * g + 4)
                    dve.tensor_tensor(r_exp[:], r_exp[:], r_max[:].unsqueeze(2).broadcast_to([P, FT, E]),
                                      ALU.mult).then_inc(sm_step, 1)
                    dve.wait_ge(sm_step, 6 * g + 5)
                    dve.tensor_copy(r_hi[:], r_exp[:]).then_inc(sm_step, 1)
                    dve.wait_ge(sm_step, 6 * g + 6)
                    for q in range(2):
                        dve.tensor_copy(rt4[:, :, 32 * q:32 * q + E], r_hi[:].bitcast(F32))
                    for q in range(2, 4):
                        last = dve.tensor_tensor(rt4[:, :, 32 * q:32 * q + E], r_exp[:], r_hi[:].bitcast(F32), ALU.subtract)
                    last.then_inc(routing_ready, 1)

                def scale(g, p, k):
                    dve.wait_ge(s_full, 8 * g + k + 1)
                    wait(dve, lo_done, 8 * g + k - 1)
                    wait(dve, hi_done, 8 * g + k - 1)
                    dve.tensor_tensor(a_f[:, k % 2, :], xT[:, p, k, :], p_s[:, k % 2, 0:FTOK], ALU.mult).then_inc(scaled, 1)

                def low(g, p, k):
                    dve.wait_ge(hi_done, 8 * g + k + 1)
                    wait(dve, m_full, 4 * g - 4)
                    dve.tensor_tensor(a_lo[:, p, k, :], a_f[:, k % 2, :], a_hi[:, p, k, :].bitcast(F32),
                                      ALU.subtract).then_inc(lo_done, 1)

                def out_stats(g, p):
                    dve.wait_ge(y_done, 4 * g + 4)
                    wait(dve, y_normed, g)
                    for t in range(FT):
                        for h in range(2):
                            last = dve.bn_stats(nst6[:, t, h, :], y[:, p, t, h * HALF:h * HALF + HALF])
                    last.then_inc(n_stats, 1)
                    dve.wait_ge(n_stats, g + 1)
                    dve.memset(wait_cell[:], 0.0)
                    for t in range(FT):
                        last = dve.bn_aggr(nmv[:, t, :], nst6[:, t])
                    last.then_inc(n_mean, 1)
                    dve.wait_ge(n_mean, g + 1)
                    wait(dve, n_rstd, g)
                    dve.tensor_scalar(nvpe[:], nmv[:, :, 1], EPS, None, ALU.add).then_inc(n_var, 1)

                def out_normalise(g, p):
                    dve.wait_ge(n_rstd, g + 1)
                    dve.wait_ge(y_stored[p], 8 * (g - p) + 16)
                    for t in range(FT):
                        last = dve.tensor_scalar(y[:, p, t, :], y[:, p, t, :], nmv[:, t, 0:1], nrstd[:, t:t + 1],
                                                 ALU.subtract, ALU.mult)
                    last.then_inc(y_normed, 1)

                for g in (0, 1):
                    stats(g, g)
                    normalise(g, g)
                dve.wait_ge(consts, 2)
                dve.wait_ge(scales_loaded, 8 * 16)
                for n, out in ((0, ics3), (1, ocs3)):
                    for q in range(4):
                        rows = slice(32 * q, 32 * q + 32)
                        last = dve.tensor_copy(out[rows, :], scale_rows[rows, n, :])
                last.then_inc(scales_split, 1)
                dve.wait_ge(scales_split, 1)
                for n, out in ((0, ics3), (1, ocs3)):
                    for q in (1, 3):
                        rows = slice(32 * q, 32 * q + 32)
                        last = dve.tensor_tensor(out[rows, :], scale_rows[rows, n, :], out[rows, :].bitcast(F32), ALU.subtract)
                last.then_inc(scales_split, 1)
                softmax(0)
                stats(2, 0)
                normalise(2, 0)
                softmax(1)
                for k in range(KD):
                    scale(0, 0, k)
                    if k:
                        low(0, 0, k - 1)
                low(0, 0, KD - 1)

                def body(g, p):
                    for q in range(4):
                        if q == 0 and exists(g + 3):
                            stats(g + 3, 1 - p)
                        if q == 0 and X is not None and exists(g - 1):
                            out_stats(g - 1, 1 - p)
                        if exists(g + 1):
                            scale(g + 1, 1 - p, 2 * q)
                            if q:
                                low(g + 1, 1 - p, 2 * q - 1)
                            scale(g + 1, 1 - p, 2 * q + 1)
                            low(g + 1, 1 - p, 2 * q)
                        if q == 0 and exists(g + 3):
                            normalise(g + 3, 1 - p)
                        if q == 1 and exists(g + 2):
                            softmax(g + 2)
                        if q == 2 and X is not None and exists(g - 1):
                            out_normalise(g - 1, 1 - p)
                        if q == 3 and exists(g + 1):
                            low(g + 1, 1 - p, KD - 1)
                        dve.wait_ge(m_full, 4 * g + q + 1)
                        dve.wait_ge(o_copied, 4 * g + q + 1)
                        if q == 0:
                            if X is not None:
                                wait(dve, n_full, 4 * g - 4)
                            else:
                                wait(dve, y_stored[p], 8 * (g - p))
                        dve.tensor_tensor(y[:, p, q // 2, q % 2 * HALF:q % 2 * HALF + HALF], p_m[:, q % 2, :],
                                          oscale[:, q % 2, :], ALU.mult).then_inc(m_scaled, 1)

                group_loop(dve, body)
                if X is not None:
                    out_stats(NG - 1, (NG - 1) % 2)
                    out_normalise(NG - 1, (NG - 1) % 2)

            @block.scalar
            def _(act):
                def copy_t(g, p, q):
                    act.wait_ge(t_full, 4 * g + q + 1)
                    wait(act, scaled, 8 * g - 16 + 2 * q + 2)
                    act.copy(xT[:, p, 2 * q:2 * q + 2, :], p_t[:].rearrange("p (k t) -> p k t", k=2)).then_inc(t_copied, 1)

                def copy_logits(g):
                    act.wait_ge(l_full, g + 1)
                    act.copy(logT[:], p_r[0:E, 0:FTOK]).then_inc(l_copied, 1)

                def exponent(g):
                    act.wait_ge(sm_step, 6 * g + 2)
                    act.activation(r_exp[:], r_exp[:], ACT.Exp).then_inc(sm_exp, 1)

                def copy_routing(g, p):
                    act.wait_ge(r_full, g + 1)
                    act.copy(rT[:, p, :], p_r[:, 0:FTOK]).then_inc(r_copied, 1)

                def high(g, p, k):
                    act.wait_ge(scaled, 8 * g + k + 1)
                    wait(act, m_full, 4 * g - 4)
                    act.copy(a_hi[:, p, k, :], a_f[:, k % 2, :]).then_inc(hi_done, 1)

                def sign_w(k):
                    act.wait_ge(w_loaded[k % 4], 16 * (k // 4 + 1))
                    act.activation(wsign[:, k, :], w_raw[:, (k % 4) // 2, k % 2, :], ACT.Sign).then_inc(w_signed, 1)

                def copy_normed(g, c):
                    act.wait_ge(n_full, 4 * g + c + 1)
                    k0 = c % 2 * 4
                    act.copy(X[:, k0:k0 + 4, bass.ds(g * FTOK + (c // 2 * P + 1), P)],
                             p_n[:].rearrange("p (k t) -> p k t", k=4)).then_inc(n_copied, 1)

                for q in range(4):
                    copy_t(0, 0, q)
                copy_logits(0)
                for q in range(4):
                    copy_t(1, 1, q)
                exponent(0)
                sign_w(0)
                sign_w(1)
                copy_routing(0, 0)
                sign_w(2)
                sign_w(3)
                copy_logits(1)
                exponent(1)
                for k in range(KD):
                    high(0, 0, k)
                    if k % 2:
                        copy_t(2, 0, k // 2)
                copy_routing(1, 1)
                for k in range(4, KD):
                    sign_w(k)

                def body(g, p):
                    for q in range(4):
                        act.wait_ge(o_full, 4 * g + q + 1)
                        wait(act, m_scaled, 4 * g + q - 1)
                        act.mul(oscale[:, q % 2, :], p_o[:], 0.5).then_inc(o_copied, 1)
                        if q == 0 and exists(g + 2):
                            copy_logits(g + 2)
                        if exists(g + 1):
                            high(g + 1, 1 - p, 2 * q)
                        if q == 3 and X is not None and exists(g - 1):
                            copy_normed(g - 1, 0)
                            copy_normed(g - 1, 1)
                        if exists(g + 1):
                            high(g + 1, 1 - p, 2 * q + 1)
                        if q == 3 and X is not None and exists(g - 1):
                            copy_normed(g - 1, 2)
                            copy_normed(g - 1, 3)
                        if q == 1 and exists(g + 2):
                            exponent(g + 2)
                        if exists(g + 3):
                            for piece in PIECES[q]:
                                copy_t(g + 3, 1 - p, piece)
                        if q == 3 and exists(g + 2):
                            copy_routing(g + 2, p)

                group_loop(act, body)
                if X is not None:
                    for c in range(4):
                        copy_normed(NG - 1, c)

            @block.tensor
            def _(pe):
                def transposes(g, p, q):
                    pe.wait_ge(x_normed, g + 1)
                    wait(pe, t_copied, 4 * g + q)
                    for c in range(2):
                        for t in range(FT):
                            k = 2 * q + c
                            last = pe.transpose(p_t[:, c * FTOK + t * P:c * FTOK + t * P + P],
                                                xin[:, p, t, k * P:k * P + P], ident[:])
                    last.then_inc(t_full, 1)

                def logits(g, p):
                    pe.wait_ge(t_copied, 4 * g + 4)
                    wait(pe, r_copied, g)
                    for k in range(KD):
                        last = pe.matmul(p_r[0:E, 0:FTOK], gateT[:, k, :], xT[:, p, k, :], start=(k == 0), stop=(k == KD - 1))
                    last.then_inc(l_full, 1)

                def logits_back(g):
                    pe.wait_ge(l_copied, g + 1)
                    for t in range(FT):
                        last = pe.matmul(p_r[:, t * E:t * E + E], logT[:, t * P:t * P + P], ident[0:E, 0:E], start=True, stop=True)
                    last.then_inc(lt_full, 1)

                def routing(g):
                    pe.wait_ge(routing_ready, g + 1)
                    for t in range(FT):
                        last = pe.transpose(p_r[:, t * P:t * P + P], rt4[:, t, :], ident[:])
                    last.then_inc(r_full, 1)

                def in_scale(g, p, k):
                    pe.wait_ge(r_copied, g + 1)
                    wait(pe, scaled, 8 * g + k - 1)
                    pe.matmul(p_s[:, k % 2, 0:FTOK], ics3[:, k * P:k * P + P], rT[:, p, :],
                              start=True, stop=True).then_inc(s_full, 1)

                def out_scale(g, p, q):
                    wait(pe, o_copied, 4 * g + q)
                    pe.matmul(p_o[:], rT[:, p, q // 2 * P:q // 2 * P + P], ocs3[:, q % 2 * HALF:q % 2 * HALF + HALF],
                              start=True, stop=True).then_inc(o_full, 1)

                def product(g, p, q, k0, k1):
                    if k0 == 0:
                        wait(pe, m_scaled, 4 * g + q - 1)
                    for k in range(k0, k1):
                        if q == 0:
                            pe.wait_ge(w_signed, k + 1)
                            pe.wait_ge(lo_done, 8 * g + k + 1)
                        for part in (a_hi, a_lo):
                            last = pe.matmul(p_m[:, q % 2, :], part[:, p, k, q // 2 * P:q // 2 * P + P],
                                             wsign[:, k, q % 2 * HALF:q % 2 * HALF + HALF],
                                             start=(k == 0 and part is a_hi), stop=(k == KD - 1 and part is a_lo))
                    if k1 == KD:
                        last.then_inc(m_full, 1)

                def normed(g, p, c):
                    pe.wait_ge(y_normed, g + 1)
                    wait(pe, n_copied, 4 * g + c)
                    for j in range(4):
                        k = c % 2 * 4 + j
                        last = pe.transpose(p_n[:, j * P:j * P + P], y[:, p, c // 2, k * P:k * P + P], ident[:])
                    last.then_inc(n_full, 1)

                for q in range(4):
                    transposes(0, 0, q)
                pe.wait_ge(gate_loaded, 16)
                logits(0, 0)
                for q in range(4):
                    transposes(1, 1, q)
                    if q == 0:
                        logits_back(0)
                routing(0)
                logits(1, 1)
                logits_back(1)
                pe.wait_ge(scales_split, 2)
                for k in range(KD):
                    in_scale(0, 0, k)
                    if k % 2:
                        transposes(2, 0, k // 2)
                routing(1)

                def body(g, p):
                    for q in range(4):
                        out_scale(g, p, q)
                        if exists(g + 1):
                            in_scale(g + 1, 1 - p, 2 * q)
                        if q == 0 and exists(g + 2):
                            logits(g + 2, p)
                        if q == 3 and X is not None and exists(g - 1):
                            for c in range(4):
                                normed(g - 1, 1 - p, c)
                                product(g, p, q, 2 * c, 2 * c + 2)
                                if c == 1 and exists(g + 1):
                                    in_scale(g + 1, 1 - p, 2 * q + 1)
                        else:
                            product(g, p, q, 0, 4)
                            if exists(g + 1):
                                in_scale(g + 1, 1 - p, 2 * q + 1)
                            if q == 0 and exists(g + 2):
                                logits_back(g + 2)
                            product(g, p, q, 4, KD)
                        if exists(g + 3):
                            for piece in PIECES[q]:
                                transposes(g + 3, 1 - p, piece)
                        if q == 3 and exists(g + 2):
                            routing(g + 2)

                group_loop(pe, body)
                if X is not None:
                    for c in range(4):
                        normed(NG - 1, (NG - 1) % 2, c)


PAIRS = T // 2
NB = PAIRS // HALF
FILTERS = [
    (-1, 1, ALU.subtract, (0,)),
    (0, 1, ALU.add, (0, 1, 2)),
    (1, 0, ALU.subtract, (0, 1, 2)),
    (0, 2, ALU.subtract, (2,)),
]
NF = len(FILTERS)
KQ = KD // 2


def conv_phase(nc, sems, conv_w, conv_b, Yd, X):
    def sem(name):
        return sems.enter_context(nc.semaphore(f"c_{name}"))

    bias_loaded = sem("bias_loaded")
    raw_loaded = [sem(f"raw_loaded{h}") for h in range(2)]
    outer_summed, tap_ready, g_hi, g_lo = sem("outer_summed"), sem("tap_ready"), sem("g_hi"), sem("g_lo")
    d_pool, d_dve, d_hi, d_lo = sem("d_pool"), sem("d_dve"), sem("d_hi"), sem("d_lo")
    chunk_used, m_added, y_stored = sem("chunk_used"), sem("m_added"), sem("y_stored")
    y_step = sem("y_step")

    with ExitStack() as ctx:
        def sb(name, shape, dt=F32):
            return ctx.enter_context(nc.sbuf_tensor(f"c_{name}", shape, dt))

        dhi = sb("dhi", [P, KD, PAIRS], F32R)
        dlo = sb("dlo", [P, KD, PAIRS], F32R)
        df = sb("df", [P, NB, HALF])
        Y = sb("Y", [P, NCH, T])
        ghi = sb("ghi", [P, 2, KQ * P], F32R)
        glo = sb("glo", [P, 2, KQ * P], F32R)
        raw = sb("raw", [P, 2, TAPS, KQ * P])
        tap = sb("tap", [P, 2, KQ * P])
        cb = sb("cb", [P, NCH])
        p_m = ctx.enter_context(nc.psum_tensor("c_p_m", [P, 2, NB, HALF], F32))
        Yp = Y[:].rearrange("p c (n e) -> p c n e", e=2)

        with nc.Block() as block:

            @block.sync
            def _(sp):
                def load(j, c, h):
                    taps = FILTERS[j][3]
                    sp.dma_start(raw[:, h, taps[0]:taps[-1] + 1, :], conv_w[c, h, :, taps[0]:taps[-1] + 1, :]).then_inc(raw_loaded[h], 16)

                sp.dma_start(cb[:], conv_b).then_inc(bias_loaded, 16)
                for j in range(NF):
                    def body(c):
                        for h in range(2):
                            wait(sp, g_lo, (j * NCH + c) * 2 + h - 1)
                            load(j, c, h)

                    body(0)
                    with sp.Fori(1, NCH) as c:
                        body(c)
                for c in range(NCH):
                    sp.wait_ge(m_added, (NF - 1) * NCH + c + 1)
                    sp.dma_start(Yd[c], Y[:, c, :]).then_inc(y_stored, 16)
                sp.wait_ge(y_stored, 16 * NCH)

            def pair_values(k, b, token):
                start = 2 * b * HALF + token + 1
                return X[:, k, start:start + 2 * HALF - 1:2]

            @block.gpsimd
            def _(pool):
                for j, (one, other, op, _) in enumerate(FILTERS):
                    for k in range(KD):
                        n = j * KD + k
                        wait(pool, d_hi, 2 * n - 1)
                        wait(pool, d_lo, 2 * n - 1)
                        if op == ALU.add:
                            pool.tensor_tensor(df[:, 0, :], pair_values(k, 0, one), pair_values(k, 0, other), ALU.add).then_inc(d_pool, 1)
                        else:
                            pool.tensor_tensor(df[:, 0, :], pair_values(k, 0, one), pair_values(k, 0, other), ALU.subtract).then_inc(d_pool, 1)

            @block.scalar
            def _(act):
                def split_data(j, k):
                    n = j * KD + k
                    if j:
                        act.wait_ge(chunk_used, (j * NCH - 1) * KD + k + 1)
                    for b, made in ((0, d_pool), (1, d_dve)):
                        act.wait_ge(made, n + 1)
                        act.copy(dhi[:, k, b * HALF:b * HALF + HALF], df[:, b, :]).then_inc(d_hi, 1)

                def split_filter(j, c, h):
                    n = (j * NCH + c) * 2 + h
                    taps = FILTERS[j][3]
                    if len(taps) == 1:
                        act.wait_ge(raw_loaded[h], 8 * (n - h) + 16)
                        source = raw[:, h, taps[0], :]
                    else:
                        act.wait_ge(tap_ready, n + 1 - 2 * NCH)
                        source = tap[:, h, :]
                    wait(act, chunk_used, 4 * n - 4)
                    act.copy(ghi[:, h, :], source).then_inc(g_hi, 1)

                for j in range(NF):
                    for h in range(2):
                        for k in range(KQ * h, KQ * h + KQ):
                            split_data(j, k)
                        split_filter(j, 0, h)
                    with act.Fori(1, NCH) as c:
                        for h in range(2):
                            split_filter(j, c, h)

            @block.vector
            def _(dve):
                def split_data(j, k):
                    one, other, op, _ = FILTERS[j]
                    n = j * KD + k
                    wait(dve, d_hi, 2 * n)
                    wait(dve, d_lo, 2 * n)
                    dve.tensor_tensor(df[:, 1, :], pair_values(k, 1, one), pair_values(k, 1, other), op).then_inc(d_dve, 1)
                    for b in range(NB):
                        dve.wait_ge(d_hi, 2 * n + b + 1)
                        cols = slice(b * HALF, b * HALF + HALF)
                        dve.tensor_tensor(dlo[:, k, cols], df[:, b, :], dhi[:, k, cols].bitcast(F32), ALU.subtract).then_inc(d_lo, 1)

                def split_filter(j, c, h):
                    n = (j * NCH + c) * 2 + h
                    taps = FILTERS[j][3]
                    if len(taps) == 1:
                        source = raw[:, h, taps[0], :]
                    else:
                        m = n - 2 * NCH
                        dve.wait_ge(raw_loaded[h], 8 * (n - h) + 16)
                        dve.tensor_tensor(raw[:, h, 0, :], raw[:, h, 0, :], raw[:, h, 2, :], ALU.add).then_inc(outer_summed, 1)
                        dve.wait_ge(outer_summed, m + 1)
                        wait(dve, g_lo, n - 1)
                        wait(dve, g_hi, n - 1)
                        dve.tensor_tensor(tap[:, h, :], raw[:, h, 0, :], raw[:, h, 1, :],
                                          ALU.add if j == 1 else ALU.subtract).then_inc(tap_ready, 1)
                        source = tap[:, h, :]
                    dve.wait_ge(g_hi, n + 1)
                    dve.tensor_tensor(glo[:, h, :], source, ghi[:, h, :].bitcast(F32), ALU.subtract).then_inc(g_lo, 1)

                def add(j, c, p):
                    n = j * NCH + c
                    m = p_m[:, p]
                    even = Yp[:, bass.ds(c, 1), :, 0]
                    odd = Yp[:, bass.ds(c, 1), :, 1]
                    even, odd = (y.rearrange("p c (b n) -> p (c b) n", b=NB) for y in (even, odd))
                    bias = cb[:, bass.ds(c, 1)]
                    dve.wait_ge(chunk_used, 8 * n + 8)
                    if j:
                        dve.wait_ge(m_added, n - NCH + 1)
                    if j == 0:
                        dve.tensor_scalar(even, m, bias, None, ALU.add).then_inc(m_added, 1)
                    if j == 1:
                        dve.tensor_scalar(odd, m, 0.5, bias, ALU.mult, ALU.add)
                        dve.scalar_tensor_tensor(even, m, 0.5, even, ALU.mult, ALU.add).then_inc(m_added, 1)
                    if j == 2:
                        dve.scalar_tensor_tensor(odd, m, -0.5, odd, ALU.mult, ALU.add)
                        dve.scalar_tensor_tensor(even, m, 0.5, even, ALU.mult, ALU.add).then_inc(m_added, 1)
                    if j == 3:
                        dve.scalar_tensor_tensor(odd, m, -1.0, odd, ALU.mult, ALU.add).then_inc(m_added, 1)

                dve.wait_ge(bias_loaded, 16)
                for j in range(NF):
                    for h in range(2):
                        for k in range(KQ * h, KQ * h + KQ):
                            split_data(j, k)
                        split_filter(j, 0, h)
                    if j:
                        add(j - 1, NCH - 1, 1)

                    def body(c, p):
                        split_filter(j, c, 0)
                        split_filter(j, c, 1)
                        add(j, c - 1, 1 - p)

                    with dve.Fori(0, (NCH - 1) // 2) as i:
                        body(2 * i + 1, 1)
                        body(2 * i + 2, 0)
                    body(NCH - 1, 1)
                add(NF - 1, NCH - 1, 1)

            @block.tensor
            def _(pe):
                def products(j, c, p):
                    n = j * NCH + c
                    wait(pe, m_added, n - 1)
                    for h in range(2):
                        pe.wait_ge(g_lo, 2 * n + h + 1)
                        for q in range(KQ):
                            k = KQ * h + q
                            pe.wait_ge(d_lo, 2 * (j * KD + k) + 2)
                            for w, parts in ((ghi, (dhi, dlo)), (glo, (dhi,))):
                                for b in range(NB):
                                    for part in parts:
                                        last = pe.matmul(p_m[:, p, b, :], w[:, h, q * P:q * P + P],
                                                         part[:, k, b * HALF:b * HALF + HALF],
                                                         start=(k == 0 and w is ghi and part is dhi), stop=(k == KD - 1 and w is glo))
                            last.then_inc(chunk_used, 1)

                for j in range(NF):
                    products(j, 0, 0)
                    products(j, 1, 1)
                    with pe.Fori(1, NCH // 2) as i:
                        products(j, 2 * i, 0)
                        products(j, 2 * i + 1, 1)


GT = 4
GTOK = GT * P
AG = T // GTOK
QUADS = H // 4
UNITS = QUADS * GT
SLOTS = 4
USE_QK0, USE_V, USE_QK, USE_WO, USE_PROJ = 0, 4, 4 + 2 * GT, 4 + 2 * GT + 4 * (QUADS - 1), 6 + 2 * GT + 4 * (QUADS - 1)
USES = USE_PROJ + 2 * GT


def attention_phase(nc, sems, Yd, x1, x2, wq, wk, wv, wo, wp, bq, bk, bv, bo, bp, ident):
    def sem(name):
        return sems.enter_context(nc.semaphore(f"a_{name}"))

    w_loaded = [sem(f"w_loaded{s}") for s in range(3)]
    bias_loaded, q_zeroed, mask_made = sem("bias_loaded"), sem("q_zeroed"), sem("mask_made")
    w_hi, w_lo = sem("w_hi"), sem("w_lo")
    y_loaded = [sem(f"y_loaded{s}") for s in range(2)]
    xs_hi, xs_lo = sem("xs_hi"), sem("xs_lo")
    gen_full, gen_free = sem("gen_full"), [sem(f"gen_free{b}") for b in range(2)]
    q_ready, k_ready, v_ready = sem("q_ready"), sem("k_ready"), sem("v_ready")
    s_full, s_masked, s_max, s_bias, exp_done = sem("s_full"), sem("s_masked"), sem("s_max"), sem("s_bias"), sem("exp_done")
    sum_inverted, probs_ready = sem("sum_inverted"), sem("probs_ready")
    pt_full, pt_copied, pv_done = sem("pt_full"), sem("pt_copied"), sem("pv_done")
    o_hi, o_lo = sem("o_hi"), sem("o_lo")
    oo_hi, oo_lo = sem("oo_hi"), sem("oo_lo")
    x_loaded, x_biased, x_summed, x_stored = ([sem(f"{n}{t}") for t in range(GT)] for n in ("x_loaded", "x_biased", "x_summed", "x_stored"))

    x1v = x1.rearrange("(g t p) d -> g t p d", p=P, t=GT)
    x2v = x2.rearrange("(g t p) d -> g t p d", p=P, t=GT)

    with ExitStack() as ctx:
        def sb(name, shape, dt=F32):
            return ctx.enter_context(nc.sbuf_tensor(f"a_{name}", shape, dt))

        def ps(name, shape):
            return ctx.enter_context(nc.psum_tensor(f"a_{name}", shape, F32))

        shapes = {"wq": (WC, HE), "wk": (WC, HE), "wv": (WC, HE), "wo": (KH, W), "wp": (WC, D)}
        hi = {n: sb(f"{n}_hi", [P, *s], F32R) for n, s in shapes.items()}
        lo = {n: sb(f"{n}_lo", [P, *s], F32R) for n, s in shapes.items()}
        xs = [sb(f"xs_{n}", [P, NCH, GTOK], F32R) for n in ("hi", "lo")]
        oo = [x[:, 2 * WC:NCH, :] for x in xs]
        yc = sb("yc", [P, 2, GTOK])
        q = sb("q", [P, 2, 2, 2, GTOK])
        kk = sb("kk", [P, 2, 2, GTOK])
        v = sb("v", [P, GT, HE])
        s = sb("s", [P, SLOTS, 4, P])
        nmx = sb("nmx", [P, SLOTS, 4])
        sums = sb("sums", [P, SLOTS, 4])
        pt = sb("pt", [P, 2, 4, P])
        oT = [sb(f"oT_{n}", [P, KH, GTOK], F32R) for n in ("hi", "lo")]
        stage = sb("stage", [P, WC * HE])
        bqs, bks, bvs, bos = sb("bqs", [P, KH]), sb("bks", [P, KH]), sb("bvs", [P, KH]), sb("bos", [P, WC])
        bps = sb("bps", [P, D])
        mask = sb("mask", [P, P])
        p_s, p_t, p_g = ps("p_s", [P, 2, HALF]), ps("p_t", [P, 2, HALF]), ps("p_g", [P, 2, HALF])
        p_o = ps("p_o", [P, 2, HALF])
        order = ["wq", "wk", "wv", "wo", "wp"]
        rooms = [stage[:], v[:, 0:2, :].rearrange("p t d -> p (t d)"), v[:, 2:4, :].rearrange("p t d -> p (t d)")]

        def parts(tensors):
            (lh, ll), (rh, rl) = tensors
            return ((lh, rh), (lh, rl), (ll, rh))

        def groups(eng, body):
            body(0, False)
            with eng.Fori(1, AG - 1) as g:
                body(g, False)
            body(AG - 1, True)

        with nc.Block() as block:

            @block.sync
            def _(sp):
                def load_y(g, c):
                    wait(sp, xs_lo, NCH * g + c - 1)
                    sp.dma_start(yc[:, c % 2, :], Yd[c, :, bass.ds(g * GTOK, GTOK)]).then_inc(y_loaded[c % 2], 16)

                def load_w(n):
                    sp.dma_start(rooms[n % 3], {"wq": wq, "wk": wk, "wv": wv, "wo": wo, "wp": wp}[order[n]]).then_inc(w_loaded[n % 3], 16)

                load_w(0)
                for to, of in ((bqs, bq), (bks, bk), (bvs, bv), (bos, bo), (bps, bp.partition_broadcast(P))):
                    sp.dma_start(to[:], of).then_inc(bias_loaded, 16)
                load_y(0, 0)
                load_y(0, 1)
                load_w(1)
                load_w(2)
                for c in range(2, NCH):
                    load_y(0, c)
                for n in (3, 4):
                    sp.wait_ge(w_lo, n - 2)
                    load_w(n)

                def body(g, last):
                    if not last:
                        for c in range(NCH):
                            load_y(g + 1, c)
                            if c == 1:
                                loads(g)
                    else:
                        loads(g)
                    for t in range(GT):
                        sp.wait_ge(x_summed[t], 2 * g + 2)
                        sp.dma_start(x2v[g, t], v[:, t, :]).then_inc(x_stored[t], 16)

                def loads(g):
                    sp.wait_ge(pv_done, UNITS * g + UNITS)
                    for t in range(GT):
                        sp.dma_start(v[:, t, :], x1v[g, t]).then_inc(x_loaded[t], 16)

                groups(sp, body)
                for t in range(GT):
                    sp.wait_ge(x_stored[t], 16 * AG)

            @block.gpsimd
            def _(pool):
                pool.memset(mask[:], 0.0).then_inc(mask_made, 1)
                pool.wait_ge(mask_made, 1)
                pool.affine_select(out=mask[:], in_=mask[:], compare_op=ALU.is_ge, fill=MASKED, base=0,
                                   pattern=[[-1, P]], channel_multiplier=1).then_inc(mask_made, 1)
                pool.memset(q[:], 0.0).then_inc(q_zeroed, 1)
                pool.wait_ge(bias_loaded, 5 * 16)

                def body(g, last):
                    for u in range(UNITS):
                        pool.wait_ge(sum_inverted, UNITS * g + u + 1)
                        r = u % SLOTS
                        pool.tensor_tensor(s[:, r], s[:, r], sums[:, r].unsqueeze(2).broadcast_to([P, 4, P]),
                                           ALU.mult).then_inc(probs_ready, 1)
                    for t in range(GT):
                        pool.wait_ge(x_loaded[t], 16 * g + 16)
                        pool.tensor_tensor(v[:, t, :], v[:, t, :], bps[:], ALU.add).then_inc(x_biased[t], 1)

                groups(pool, body)

            @block.scalar
            def _(act):
                def split_high(g, c):
                    act.wait_ge(y_loaded[c % 2], 48 * g + 16 * (c // 2) + 16)
                    wait(act, gen_full, USES * (g - 1) + (USE_WO if c < 2 * WC else USES))
                    act.copy(xs[0][:, c, :], yc[:, c % 2, :]).then_inc(xs_hi, 1)

                def weight_high(n):
                    act.wait_ge(w_loaded[n % 3], 16 * (n // 3 + 1))
                    w = hi[order[n]]
                    act.copy(w[:].rearrange("p c n -> p (c n)"), rooms[n % 3]).then_inc(w_hi, 1)

                def take_q(g, quad, part, use):
                    act.wait_ge(gen_full, USES * g + use + 1)
                    wait(act, s_full, UNITS * g + 4 * quad - 4)
                    i = part // 2
                    for head in range(2):
                        rows = slice(DH * head, DH * head + DH)
                        last = act.activation(q[rows, quad % 2, i, head, :], p_g[rows, use % 2, :], ACT.Identity,
                                              bias=bqs[rows, 2 * quad + i:2 * quad + i + 1])
                    last.then_inc(q_ready, 1)

                def take_v(g, n):
                    use = USE_V + n
                    act.wait_ge(gen_full, USES * g + use + 1)
                    wait(act, x_stored[n // 2], 16 * g)
                    act.copy(v[:, n // 2, n % 2 * HALF:n % 2 * HALF + HALF], p_g[:, use % 2, :]).then_inc(v_ready, 1)

                for c in range(2):
                    split_high(0, c)
                weight_high(0)
                for c in range(2, 4):
                    split_high(0, c)
                weight_high(1)
                weight_high(2)
                for c in range(4, NCH):
                    split_high(0, c)
                act.wait_ge(bias_loaded, 5 * 16)
                act.wait_ge(q_zeroed, 1)
                weight_high(3)
                weight_high(4)
                act.wait_ge(w_lo, 5)

                def body(g, last):
                    take_q(g, 0, 0, USE_QK0)
                    take_q(g, 0, 2, USE_QK0 + 2)
                    for n in range(2 * GT):
                        take_v(g, n)
                    for u in range(UNITS + 3):
                        if u < UNITS - 4 and u % 2 == 0:
                            take_q(g, u // 4 + 1, u % 4, USE_QK + u)
                        if u < UNITS:
                            act.wait_ge(s_bias, UNITS * g + u + 1)
                            r = u % SLOTS
                            for h in range(4):
                                done = act.activation(s[:, r, h, :], s[:, r, h, :], ACT.Exp, bias=nmx[:, r, h:h + 1],
                                                      scale=SCALE, accum_out=sums[:, r, h:h + 1])
                            done.then_inc(exp_done, 1)
                        if 2 <= u < UNITS + 2:
                            act.wait_ge(pt_full, UNITS * g + u - 1)
                            wait(act, pv_done, UNITS * g + u - 3)
                            act.copy(pt[:, u % 2].rearrange("p h t -> p (h t)"), p_t[:, u % 2, :]).then_inc(pt_copied, 1)
                        if u >= 6 and (u - 6) % 4 == 0:
                            quad = (u - 6) // 4
                            act.wait_ge(pv_done, UNITS * g + 4 * quad + 4)
                            wait(act, gen_full, USES * (g - 1) + USE_PROJ)
                            for i in range(2):
                                act.activation(oT[0][:, 2 * quad + i, :], p_o[:, i, :], ACT.Identity,
                                               bias=bvs[:, 2 * quad + i:2 * quad + i + 1]).then_inc(o_hi, 1)
                    if not last:
                        for c in range(2 * WC):
                            split_high(g + 1, c)
                    for m in range(WC):
                        use = USE_WO + m
                        act.wait_ge(gen_full, USES * g + use + 1)
                        act.activation(oo[0][:, m, :], p_g[:, use % 2, :], ACT.Identity, bias=bos[:, m:m + 1]).then_inc(oo_hi, 1)
                    if not last:
                        for c in range(2 * WC, NCH):
                            split_high(g + 1, c)

                groups(act, body)

            @block.vector
            def _(dve):
                def split_low(g, c):
                    dve.wait_ge(xs_hi, NCH * g + c + 1)
                    dve.tensor_tensor(xs[1][:, c, :], yc[:, c % 2, :], xs[0][:, c, :].bitcast(F32), ALU.subtract).then_inc(xs_lo, 1)

                def weight_low(n):
                    dve.wait_ge(w_hi, n + 1)
                    a, b = (w[order[n]][:].rearrange("p c n -> p (c n)") for w in (hi, lo))
                    dve.tensor_tensor(b, rooms[n % 3], a.bitcast(F32), ALU.subtract).then_inc(w_lo, 1)

                def take_k(g, quad, part, use):
                    dve.wait_ge(gen_full, USES * g + use + 1)
                    wait(dve, s_full, UNITS * g + 4 * quad - 4)
                    i = part // 2
                    dve.tensor_scalar(kk[:, quad % 2, i, :], p_g[:, use % 2, :], bks[:, 2 * quad + i:2 * quad + i + 1], None,
                                      ALU.add).then_inc(k_ready, 1)

                for c in range(2):
                    split_low(0, c)
                weight_low(0)
                for c in range(2, 4):
                    split_low(0, c)
                weight_low(1)
                weight_low(2)
                for c in range(4, NCH):
                    split_low(0, c)
                dve.wait_ge(bias_loaded, 5 * 16)
                weight_low(3)
                weight_low(4)
                dve.wait_ge(mask_made, 2)

                def body(g, last):
                    take_k(g, 0, 1, USE_QK0 + 1)
                    take_k(g, 0, 3, USE_QK0 + 3)
                    for u in range(UNITS + 3):
                        if u < UNITS - 4 and u % 2 == 1:
                            take_k(g, u // 4 + 1, u % 4, USE_QK + u)
                        if u < UNITS:
                            n, r = UNITS * g + u, u % SLOTS
                            dve.wait_ge(s_full, n + 1)
                            wait(dve, pt_full, n - SLOTS + 1)
                            dve.tensor_tensor(s[:, r], p_s[:, u % 2, :].rearrange("p (h t) -> p h t", h=4),
                                              mask[:].unsqueeze(1).broadcast_to([P, 4, P]), ALU.add).then_inc(s_masked, 1)
                            dve.wait_ge(s_masked, n + 1)
                            dve.tensor_reduce(sums[:, r], s[:, r], AX.X, ALU.max).then_inc(s_max, 1)
                            dve.wait_ge(s_max, n + 1)
                            dve.tensor_scalar(nmx[:, r], sums[:, r], -SCALE, None, ALU.mult).then_inc(s_bias, 1)
                        if 1 <= u <= UNITS:
                            n, r = UNITS * g + u - 1, (u - 1) % SLOTS
                            dve.wait_ge(exp_done, n + 1)
                            dve.reciprocal(sums[:, r], sums[:, r]).then_inc(sum_inverted, 1)
                        if u >= 6 and (u - 6) % 4 == 0:
                            quad = (u - 6) // 4
                            for i in range(2):
                                c = 2 * quad + i
                                dve.wait_ge(o_hi, KH * g + c + 1)
                                dve.scalar_tensor_tensor(oT[1][:, c, :], p_o[:, i, :], bvs[:, c:c + 1], oT[0][:, c, :].bitcast(F32),
                                                         ALU.add, ALU.subtract).then_inc(o_lo, 1)
                    if not last:
                        for c in range(2 * WC):
                            split_low(g + 1, c)
                    for m in range(WC):
                        use = USE_WO + m
                        dve.wait_ge(oo_hi, WC * g + m + 1)
                        dve.scalar_tensor_tensor(oo[1][:, m, :], p_g[:, use % 2, :], bos[:, m:m + 1], oo[0][:, m, :].bitcast(F32),
                                                 ALU.add, ALU.subtract).then_inc(oo_lo, 1)
                    for n in range(2 * GT):
                        use, t = USE_PROJ + n, n // 2
                        dve.wait_ge(gen_full, USES * g + use + 1)
                        dve.wait_ge(x_biased[t], g + 1)
                        cols = slice(n % 2 * HALF, n % 2 * HALF + HALF)
                        dve.tensor_tensor(v[:, t, cols], p_g[:, use % 2, :], v[:, t, cols], ALU.add).then_inc(x_summed[t], 1)
                    if not last:
                        for c in range(2 * WC, NCH):
                            split_low(g + 1, c)

                groups(dve, body)

            @block.tensor
            def _(pe):
                def use_bank(g, use):
                    before = use - 2 if use >= 2 else use - 2 + USES
                    g = g if use >= 2 else g - 1
                    if before < USE_V:
                        queries = before % 2 == 0
                        wait(pe, q_ready if queries else k_ready, 2 * QUADS * g + before // 2 + 1)
                    elif before < USE_QK:
                        wait(pe, v_ready, 2 * GT * g + before - USE_V + 1)
                    elif before < USE_WO:
                        queries = before % 2 == 0
                        wait(pe, q_ready if queries else k_ready, 2 * QUADS * g + 2 + (before - USE_QK) // 2 + 1)
                    elif before < USE_PROJ:
                        wait(pe, oo_lo, WC * g + before - USE_WO + 1)
                    else:
                        n = before - USE_PROJ
                        wait(pe, x_summed[n // 2], 2 * g + n % 2 + 1)

                def qk(g, quad, part, use):
                    use_bank(g, use)
                    name, c0 = (("wq", 0), ("wk", WC))[part % 2]
                    he = 2 * quad + part // 2
                    for c in range(WC):
                        for n, (a, b) in enumerate(parts(((hi[name], lo[name]), xs))):
                            mm = pe.matmul(p_g[:, use % 2, :], a[:, c, he * P:he * P + P], b[:, c0 + c, :],
                                           start=(c == 0 and n == 0), stop=(c == WC - 1 and n == 2))
                    mm.then_inc(gen_full, 1)

                def body(g, last):
                    pe.wait_ge(xs_lo, NCH * g + 2 * WC)
                    for part in range(4):
                        qk(g, 0, part, USE_QK0 + part)
                    pe.wait_ge(xs_lo, NCH * g + NCH)
                    for n in range(2 * GT):
                        use, t, cols = USE_V + n, n // 2, slice(n % 2 * HALF, n % 2 * HALF + HALF)
                        use_bank(g, use)
                        for c in range(WC):
                            for i, (a, b) in enumerate(parts((xs, (hi["wv"], lo["wv"])))):
                                mm = pe.matmul(p_g[:, use % 2, :], a[:, 2 * WC + c, t * P:t * P + P], b[:, c, cols],
                                               start=(c == 0 and i == 0), stop=(c == WC - 1 and i == 2))
                        mm.then_inc(gen_full, 1)
                    for u in range(UNITS + 3):
                        if u < UNITS:
                            quad, t = u // GT, u % GT
                            pe.wait_ge(q_ready, 2 * QUADS * g + 2 * quad + 2)
                            pe.wait_ge(k_ready, 2 * QUADS * g + 2 * quad + 2)
                            wait(pe, s_masked, UNITS * g + u - 1)
                            for h in range(4):
                                mm = pe.matmul(p_s[:, u % 2, h * P:h * P + P], q[:, quad % 2, h // 2, h % 2, t * P:t * P + P],
                                               kk[:, quad % 2, h // 2, t * P:t * P + P], start=True, stop=True)
                            mm.then_inc(s_full, 1)
                        if u < UNITS - 4:
                            qk(g, u // 4 + 1, u % 4, USE_QK + u)
                        if 2 <= u < UNITS + 2:
                            w = u - 2
                            pe.wait_ge(probs_ready, UNITS * g + w + 1)
                            wait(pe, pt_copied, UNITS * g + w - 1)
                            for h in range(4):
                                mm = pe.transpose(p_t[:, w % 2, h * P:h * P + P], s[:, w % SLOTS, h, :], ident[:])
                            mm.then_inc(pt_full, 1)
                        if u >= 3:
                            w = u - 3
                            quad, t = w // GT, w % GT
                            pe.wait_ge(pt_copied, UNITS * g + w + 1)
                            if w == 0:
                                pe.wait_ge(v_ready, 2 * GT * g + 2 * GT)
                            if t == 0:
                                wait(pe, o_lo, KH * g + 2 * quad)
                            for h in range(4):
                                head = 4 * quad + h
                                mm = pe.matmul(p_o[DH * (h % 2):DH * (h % 2) + DH, h // 2, t * P:t * P + P],
                                               v[:, t, head * DH:head * DH + DH], pt[:, w % 2, h, :], start=True, stop=True)
                            mm.then_inc(pv_done, 1)
                    pe.wait_ge(w_lo, 5)
                    for m in range(WC):
                        use = USE_WO + m
                        use_bank(g, use)
                        for c in range(KH):
                            pe.wait_ge(o_lo, KH * g + c + 1)
                            for n, (a, b) in enumerate(parts(((hi["wo"], lo["wo"]), oT))):
                                mm = pe.matmul(p_g[:, use % 2, :], a[:, c, m * P:m * P + P], b[:, c, :],
                                               start=(c == 0 and n == 0), stop=(c == KH - 1 and n == 2))
                        mm.then_inc(gen_full, 1)
                    pe.wait_ge(oo_lo, WC * g + WC)
                    for i in range(2 * GT):
                        use, t, cols = USE_PROJ + i, i // 2, slice(i % 2 * HALF, i % 2 * HALF + HALF)
                        use_bank(g, use)
                        for c in range(WC):
                            for n, (a, b) in enumerate(parts((oo, (hi["wp"], lo["wp"])))):
                                mm = pe.matmul(p_g[:, use % 2, :], a[:, c, t * P:t * P + P], b[:, c, cols],
                                               start=(c == 0 and n == 0), stop=(c == WC - 1 and n == 2))
                        mm.then_inc(gen_full, 1)

                pe.wait_ge(q_zeroed, 1)
                pe.wait_ge(w_lo, 3)
                groups(pe, body)


def macaron_kernel(nc, x, conv_w, conv_b, wq, bq, wk, bk, wv, bv, wo, bo, wp, bp, w_t, bias, gate_t, ics, ocs, out):
    x1 = nc.dram_tensor("x_after_ffn1", (T, D), F32).ap()
    x2 = nc.dram_tensor("x_after_attention", (T, D), F32).ap()
    conv_out = nc.dram_tensor("conv_out", (NCH, P, T), F32).ap()

    with ExitStack() as sems, ExitStack() as ctx:
        ident = ctx.enter_context(nc.sbuf_tensor("ident", [P, P], F32))
        zeroed = sems.enter_context(nc.semaphore("zeroed"))

        with nc.Block() as block:
            @block.gpsimd
            def _(pool):
                pool.memset(ident[:], 0.0).then_inc(zeroed, 1)
                pool.wait_ge(zeroed, 1)
                pool.affine_select(out=ident[:], in_=ident[:], compare_op=ALU.not_equal, fill=1.0, base=0,
                                   pattern=[[-1, P]], channel_multiplier=1)

        with nc.sbuf_tensor("X", [P, KD, T + 2], F32) as X:
            ffn_phase(nc, sems, "f1", x, x1, w_t, bias, gate_t, ics, ocs, ident, X)
            conv_phase(nc, sems, conv_w, conv_b, conv_out, X)
        attention_phase(nc, sems, conv_out, x1, x2, wq, wk, wv, wo, wp, bq, bk, bv, bo, bp, ident)
        ffn_phase(nc, sems, "f2", x2, out, w_t, bias, gate_t, ics, ocs, ident, None)


def kernel(**inputs):
    import numpy as _np
    import concourse.bacc as _bacc
    from concourse import mybir as _mybir
    from concourse.bass_utils import run_bass_kernel_spmd as _run

    a = {n.removeprefix("L0_"): _np.asarray(v) for n, v in inputs.items()}

    def chunked(w, n):
        return w.reshape(n, P, -1).transpose(1, 0, 2).reshape(P, -1)

    def columns(b):
        return b.reshape(-1, P).T

    laid = {
        "x": a["attn_inputs"].reshape(T, D),
        "conv_w": a["attn_conv_w"].reshape(TAPS, 2, KQ, P, NCH, P).transpose(4, 1, 3, 0, 2, 5).reshape(NCH, 2, P, TAPS, KQ * P),
        "conv_b": columns(a["attn_conv_b"]),
        "wq": chunked(a["attn_wq"], WC), "bq": columns(a["attn_bq"]),
        "wk": chunked(a["attn_wk"], WC), "bk": columns(a["attn_bk"]),
        "wv": chunked(a["attn_wv"], WC), "bv": columns(a["attn_bv"]),
        "wo": chunked(a["attn_wo"].reshape(HE, W), KH), "bo": columns(a["attn_bo"]),
        "wp": chunked(a["attn_proj_w"], WC), "bp": a["attn_proj_b"],
        "w_t": a["ffn_weight"].T, "bias": a["ffn_bias"], "gate_t": a["ffn_gate_w"].T,
        "ics": a["ffn_in_channel_scale"], "ocs": a["ffn_out_channel_scale"],
    }
    nc = _bacc.Bacc("TRN2", target_bir_lowering=False, num_devices=1)
    arrays, args = {}, []
    for name, value in laid.items():
        value = _np.ascontiguousarray(value)
        arrays[f"in_{name}_dram"] = value
        args.append(nc.dram_tensor(f"in_{name}_dram", value.shape, _mybir.dt.from_np(value.dtype), kind="ExternalInput").ap())
    args.append(nc.dram_tensor("out_0_dram", (T, D), _mybir.dt.float32, kind="ExternalOutput").ap())
    macaron_kernel(nc, *args)
    r = _run(nc, [arrays], core_ids=[0])
    return r.results[0]["out_0_dram"].reshape(1, T, D)
```

```python
from contextlib import ExitStack

import concourse.bass as bass
from concourse import mybir

F32 = mybir.dt.float32
F32R = mybir.dt.float32r
ALU = mybir.AluOpType
ACT = mybir.ActivationFunctionType
AX = mybir.AxisListType

P = 128
T = 2048
D = 1024
KD = D // P
E = 8
W = 256
WC = W // P
NCH = 3 * WC
TAPS = 3
H = 16
DH = 64
HE = H * DH
KH = HE // P
EPS = 1e-5
MASKED = -8e9
SCALE = 0.125
HALF = 512
FTOK = 256
FT = FTOK // P
NG = T // FTOK
PIECES = [[], [0], [1], [2, 3]]


def wait(eng, sem, value):
    if not isinstance(value, int) or value > 0:
        eng.wait_ge(sem, value)


def group_loop(eng, body):
    body(0, 0)
    with eng.Fori(0, (NG - 4) // 2) as i:
        body(2 * i + 1, 1)
        body(2 * i + 2, 0)
    for g in range(NG - 3, NG):
        body(g, g % 2)


def first_round(g):
    return isinstance(g, int) and g == 0


def early(g):
    return isinstance(g, int) and g < 2


def late(g):
    return isinstance(g, int) and g == NG - 1


def exists(g):
    return not isinstance(g, int) or 0 <= g < NG


def ffn_phase(nc, sems, tag, src, dst, w_t, bias, gate_t, ics, ocs, ident, X):
    def sem(name):
        return sems.enter_context(nc.semaphore(f"{tag}_{name}"))

    first_loaded = sem("first_loaded")
    x_loaded = [sem(f"x_loaded{p}") for p in range(2)]
    w_loaded = [sem(f"w_loaded{s}") for s in range(4)]
    gate_loaded, bias_loaded = sem("gate_loaded"), sem("bias_loaded")
    scales_zeroed, scales_loaded = sem("scales_zeroed"), sem("scales_loaded")
    scales_split = sem("scales_split")
    w_signed = sem("w_signed")
    consts = sem("consts")
    bias_halved = sem("bias_halved")
    ln_stats, ln_mean, ln_var, ln_rstd, x_normed = (sem(n) for n in ("ln_stats", "ln_mean", "ln_var", "ln_rstd", "x_normed"))
    t_full, t_copied = sem("t_full"), sem("t_copied")
    l_full, l_copied, lt_full = sem("l_full"), sem("l_copied"), sem("lt_full")
    sm_step, sm_exp, routing_ready = sem("sm_step"), sem("sm_exp"), sem("routing_ready")
    r_full, r_copied = sem("r_full"), sem("r_copied")
    s_full, scaled, hi_done, lo_done = sem("s_full"), sem("scaled"), sem("hi_done"), sem("lo_done")
    o_full, o_copied = sem("o_full"), sem("o_copied")
    m_full, m_scaled = sem("m_full"), sem("m_scaled")
    res_loaded = [sem(f"res_loaded{t}") for t in range(FT)]
    res_biased, y_done = sem("res_biased"), sem("y_done")
    y_stored = [sem(f"y_stored{p}") for p in range(2)]
    if X is not None:
        n_stats, n_mean, n_var, n_rstd, y_normed = (sem(n) for n in ("n_stats", "n_mean", "n_var", "n_rstd", "y_normed"))
        n_full, n_copied = sem("n_full"), sem("n_copied")

    srcv = src.rearrange("(g t p) d -> g p t d", p=P, t=FT)
    dstv = dst.rearrange("(g t p) d -> g p t d", p=P, t=FT)
    wv = w_t.rearrange("(k p) o -> k p o", p=P)

    with ExitStack() as ctx:
        def sb(name, shape, dt=F32):
            return ctx.enter_context(nc.sbuf_tensor(f"{tag}_{name}", shape, dt))

        def ps(name, shape):
            return ctx.enter_context(nc.psum_tensor(f"{tag}_{name}", shape, F32))

        wsign = sb("wsign", [P, KD, D], F32R)
        a_hi = sb("a_hi", [P, 2, KD, FTOK], F32R)
        a_lo = sb("a_lo", [P, 2, KD, FTOK], F32R)
        a_f = sb("a_f", [P, 2, FTOK])
        xT = sb("xT", [P, 2, KD, FTOK])
        xin = sb("xin", [P, 2, FT, D])
        y = sb("y", [P, 2, FT, D])
        res = sb("res", [P, FT, D])
        oscale = sb("oscale", [P, 2, HALF])
        ics3 = sb("ics3", [P, D], F32R)
        ocs3 = sb("ocs3", [P, D], F32R)
        hbias = sb("hbias", [P, D])
        gateT = sb("gateT", [P, KD, E])
        logT = sb("logT", [E, FTOK])
        rt4 = sb("rt4", [P, FT, P])
        rT = sb("rT", [P, 2, FTOK], F32R)
        r_max = sb("r_max", [P, FT])
        r_exp = sb("r_exp", [P, FT, E])
        r_sum = sb("r_sum", [P, FT])
        r_hi = sb("r_hi", [P, FT, E], F32R)
        st6 = sb("st6", [P, FT, 2, 6])
        mv = sb("mv", [P, FT, 2])
        vpe = sb("vpe", [P, FT])
        rstd = sb("rstd", [P, FT])
        minus_half = sb("minus_half", [P, FT])
        nst6 = sb("nst6", [P, FT, 2, 6])
        nmv = sb("nmv", [P, FT, 2])
        nvpe = sb("nvpe", [P, FT])
        nrstd = sb("nrstd", [P, FT])
        wait_cell = sb("wait_cell", [P, 1])
        start_cells = sb("start_cells", [P, 6])
        minus_low = sb("minus_low", [P, 1])
        scale_rows = res
        w_raw = y

        p_t = ps("p_t", [P, HALF])
        p_n = ps("p_n", [P, HALF])
        p_r = ps("p_r", [P, HALF])
        p_o = ps("p_o", [P, HALF])
        p_s = ps("p_s", [P, 2, HALF])
        p_m = ps("p_m", [P, 2, HALF])

        with nc.Block() as block:

            @block.sync
            def _(sp):
                def load_x(g, p):
                    sp.dma_start(xin[:, p], srcv[g]).then_inc(x_loaded[p], 16)

                def load_w(k):
                    sp.dma_start(w_raw[:, (k % 4) // 2, k % 2, :], wv[k]).then_inc(w_loaded[k % 4], 16)

                def load_res(g, t):
                    sp.dma_start(res[:, t, :], srcv[g][:, t, :]).then_inc(res_loaded[t], 16)

                sp.dma_start(xin[:, 0, 0, :], srcv[0][:, 0, :]).then_inc(first_loaded, 16)
                sp.dma_start(xin[:, 0, 1, :], srcv[0][:, 1, :]).then_inc(x_loaded[0], 16)
                load_x(1, 1)
                sp.dma_start(gateT[:], gate_t.rearrange("(k p) e -> p k e", p=P)).then_inc(gate_loaded, 16)
                sp.wait_ge(scales_zeroed, 1)
                for q in range(4):
                    sp.dma_start(scale_rows[32 * q:32 * q + E, 0, :], ics).then_inc(scales_loaded, 16)
                    sp.dma_start(scale_rows[32 * q:32 * q + E, 1, :], ocs).then_inc(scales_loaded, 16)
                for k in range(4):
                    load_w(k)
                sp.dma_start(hbias[:], bias.partition_broadcast(P)).then_inc(bias_loaded, 16)
                sp.wait_ge(t_full, 4)
                load_x(2, 0)
                for k in range(4, KD):
                    sp.wait_ge(w_signed, k - 3)
                    load_w(k)
                sp.wait_ge(scales_split, 6)
                for t in range(FT):
                    load_res(0, t)

                def store(g, p):
                    sp.wait_ge(y_done, 4 * g + 4)
                    sp.dma_start(dstv[g], y[:, p]).then_inc(y_stored[p], 16)

                def body(g, p):
                    if exists(g + 3):
                        sp.wait_ge(t_full, 4 * g + 8)
                        load_x(g + 3, 1 - p)
                    if exists(g - 1):
                        for t in range(FT):
                            sp.wait_ge(y_done, 4 * g - 2 + 2 * t)
                            load_res(g, t)
                        store(g - 1, 1 - p)

                group_loop(sp, body)
                store(NG - 1, (NG - 1) % 2)
                sp.wait_ge(y_stored[0], 16 * (NG // 2) + 1)
                sp.wait_ge(y_stored[1], 16 * (NG // 2) + 1)

            @block.gpsimd
            def _(pool):
                pool.memset(scale_rows[:], 0.0).then_inc(scales_zeroed, 1)
                pool.memset(minus_half[:], -0.5).then_inc(consts, 1)
                pool.memset(rt4[:], 0.0).then_inc(consts, 1)
                if X is not None:
                    pool.memset(X[:, :, 0:1], 0.0).then_inc(consts, 1)
                    pool.memset(X[:, :, T + 1:T + 2], 0.0).then_inc(consts, 1)
                def power(g):
                    wait(pool, x_normed, g)
                    pool.wait_ge(ln_var, g + 1)
                    pool.tensor_tensor(rstd[:], vpe[:], minus_half[:], ALU.pow).then_inc(ln_rstd, 1)

                pool.wait_ge(consts, 1)
                power(0)
                power(1)
                pool.wait_ge(bias_loaded, 16)
                pool.tensor_scalar(hbias[:], hbias[:], 0.5, None, ALU.mult).then_inc(bias_halved, 1)
                power(2)
                pool.wait_ge(bias_halved, 1)

                def body(g, p):
                    if exists(g + 3):
                        power(g + 3)
                    if X is not None and exists(g - 1):
                        pool.wait_ge(n_var, g)
                        pool.tensor_tensor(nrstd[:], nvpe[:], minus_half[:], ALU.pow).then_inc(n_rstd, 1)
                    for q in range(4):
                        t, h = q // 2, slice(q % 2 * HALF, q % 2 * HALF + HALF)
                        pool.wait_ge(res_loaded[t], 16 * g + 16)
                        pool.tensor_tensor(res[:, t, h], res[:, t, h], hbias[:, h], ALU.add).then_inc(res_biased, 1)
                        pool.wait_ge(res_biased, 4 * g + q + 1)
                        pool.wait_ge(m_scaled, 4 * g + q + 1)
                        pool.tensor_tensor(y[:, p, t, h], y[:, p, t, h], res[:, t, h], ALU.add).then_inc(y_done, 1)

                group_loop(pool, body)
                if X is not None:
                    pool.wait_ge(n_var, NG)
                    pool.tensor_tensor(nrstd[:], nvpe[:], minus_half[:], ALU.pow).then_inc(n_rstd, 1)

            @block.vector
            def _(dve):
                def stats(g, p):
                    wait(dve, x_normed, g)
                    if first_round(g):
                        dve.wait_ge(first_loaded, 16)
                    else:
                        dve.wait_ge(x_loaded[p], 8 * (g - p) + 16)
                    for t in range(FT):
                        if first_round(g) and t:
                            dve.wait_ge(x_loaded[p], 16)
                        for h in range(2):
                            last = dve.bn_stats(st6[:, t, h, :], xin[:, p, t, h * HALF:h * HALF + HALF])
                    last.then_inc(ln_stats, 1)
                    dve.wait_ge(ln_stats, g + 1)
                    dve.memset(wait_cell[:], 0.0)
                    for t in range(FT):
                        last = dve.bn_aggr(mv[:, t, :], st6[:, t])
                    last.then_inc(ln_mean, 1)
                    dve.wait_ge(ln_mean, g + 1)
                    wait(dve, ln_rstd, g)
                    dve.tensor_scalar(vpe[:], mv[:, :, 1], EPS, None, ALU.add).then_inc(ln_var, 1)

                def normalise(g, p):
                    dve.wait_ge(ln_rstd, g + 1)
                    for t in range(FT):
                        last = dve.tensor_scalar(xin[:, p, t, :], xin[:, p, t, :], mv[:, t, 0:1], rstd[:, t:t + 1],
                                                 ALU.subtract, ALU.mult)
                    last.then_inc(x_normed, 1)

                def softmax(g):
                    log = p_r[:, 0:FT * E].rearrange("p (t e) -> p t e", t=FT)
                    dve.wait_ge(lt_full, g + 1)
                    wait(dve, r_full, g)
                    dve.tensor_reduce(r_max[:], log, AX.X, ALU.max).then_inc(sm_step, 1)
                    dve.wait_ge(sm_step, 6 * g + 1)
                    dve.tensor_tensor(r_exp[:], log, r_max[:].unsqueeze(2).broadcast_to([P, FT, E]),
                                      ALU.subtract).then_inc(sm_step, 1)
                    dve.wait_ge(sm_exp, g + 1)
                    dve.tensor_reduce(r_sum[:], r_exp[:], AX.X, ALU.add).then_inc(sm_step, 1)
                    dve.wait_ge(sm_step, 6 * g + 3)
                    dve.reciprocal(r_max[:], r_sum[:]).then_inc(sm_step, 1)
                    dve.wait_ge(sm_step, 6 * g + 4)
                    dve.tensor_tensor(r_exp[:], r_exp[:], r_max[:].unsqueeze(2).broadcast_to([P, FT, E]),
                                      ALU.mult).then_inc(sm_step, 1)
                    dve.wait_ge(sm_step, 6 * g + 5)
                    dve.tensor_copy(r_hi[:], r_exp[:]).then_inc(sm_step, 1)
                    dve.wait_ge(sm_step, 6 * g + 6)
                    for q in range(2):
                        dve.tensor_copy(rt4[:, :, 32 * q:32 * q + E], r_hi[:].bitcast(F32))
                    for q in range(2, 4):
                        last = dve.tensor_tensor(rt4[:, :, 32 * q:32 * q + E], r_exp[:], r_hi[:].bitcast(F32), ALU.subtract)
                    last.then_inc(routing_ready, 1)

                def scale(g, p, k):
                    dve.wait_ge(s_full, 8 * g + k + 1)
                    wait(dve, lo_done, 8 * g + k - 1)
                    wait(dve, hi_done, 8 * g + k - 1)
                    dve.tensor_tensor(a_f[:, k % 2, :], xT[:, p, k, :], p_s[:, k % 2, 0:FTOK], ALU.mult).then_inc(scaled, 1)

                def low(g, p, k):
                    dve.wait_ge(hi_done, 8 * g + k + 1)
                    wait(dve, m_full, 4 * g - 4)
                    dve.tensor_tensor(a_lo[:, p, k, :], a_f[:, k % 2, :], a_hi[:, p, k, :].bitcast(F32),
                                      ALU.subtract).then_inc(lo_done, 1)

                def out_stats(g, p):
                    dve.wait_ge(y_done, 4 * g + 4)
                    wait(dve, y_normed, g + 1)
                    for t in range(FT):
                        for h in range(2):
                            last = dve.bn_stats(nst6[:, t, h, :], y[:, p, t, h * HALF:h * HALF + HALF])
                    last.then_inc(n_stats, 1)
                    dve.wait_ge(n_stats, g + 1)
                    dve.memset(wait_cell[:], 0.0)
                    for t in range(FT):
                        last = dve.bn_aggr(nmv[:, t, :], nst6[:, t])
                    last.then_inc(n_mean, 1)
                    dve.wait_ge(n_mean, g + 1)
                    wait(dve, n_rstd, g + 1)
                    dve.tensor_scalar(nvpe[:], nmv[:, :, 1], EPS, None, ALU.add).then_inc(n_var, 1)

                def out_normalise(g, p):
                    dve.wait_ge(n_rstd, g + 2)
                    dve.wait_ge(y_stored[p], 8 * (g - p) + 17)
                    for t in range(FT):
                        last = dve.tensor_scalar(y[:, p, t, :], y[:, p, t, :], nmv[:, t, 0:1], nrstd[:, t:t + 1],
                                                 ALU.subtract, ALU.mult)
                    last.then_inc(y_normed, 1)

                started = y_stored + ([n_full, n_copied, n_rstd, y_normed] if X is not None else [])
                for n, count in enumerate(started):
                    dve.memset(start_cells[:, n:n + 1], 0.0).then_inc(count, 1)
                for q in range(4):
                    dve.memset(minus_low[32 * q:32 * q + 32, :], -1.0 if q % 2 else 0.0).then_inc(scales_split, 1)
                for g in (0, 1):
                    stats(g, g)
                    normalise(g, g)
                dve.wait_ge(consts, 2)
                dve.wait_ge(scales_split, 4)
                dve.wait_ge(scales_loaded, 8 * 16)
                for n, out in ((0, ics3), (1, ocs3)):
                    last = dve.tensor_copy(out[:], scale_rows[:, n, :])
                last.then_inc(scales_split, 1)
                dve.wait_ge(scales_split, 5)
                for n, out in ((0, ics3), (1, ocs3)):
                    last = dve.scalar_tensor_tensor(out[:], out[:].bitcast(F32), minus_low[:, 0:1], scale_rows[:, n, :],
                                                    ALU.mult, ALU.add)
                last.then_inc(scales_split, 1)
                softmax(0)
                stats(2, 0)
                for k in range(KD):
                    scale(0, 0, k)
                    if k:
                        low(0, 0, k - 1)
                low(0, 0, KD - 1)
                normalise(2, 0)
                softmax(1)

                def body(g, p):
                    for q in range(4):
                        if q == 0 and exists(g + 3):
                            stats(g + 3, 1 - p)
                        if q == 0 and X is not None and exists(g - 1):
                            out_stats(g - 1, 1 - p)
                        if exists(g + 1):
                            scale(g + 1, 1 - p, 2 * q)
                            if q:
                                low(g + 1, 1 - p, 2 * q - 1)
                            scale(g + 1, 1 - p, 2 * q + 1)
                            low(g + 1, 1 - p, 2 * q)
                        if q == 0 and exists(g + 3):
                            normalise(g + 3, 1 - p)
                        if q == 1 and exists(g + 2):
                            softmax(g + 2)
                        if q == 2 and X is not None and exists(g - 1):
                            out_normalise(g - 1, 1 - p)
                        if q == 3 and exists(g + 1):
                            low(g + 1, 1 - p, KD - 1)
                        dve.wait_ge(m_full, 4 * g + q + 1)
                        dve.wait_ge(o_copied, 4 * g + q + 1)
                        if q == 0:
                            if X is not None:
                                wait(dve, n_full, 4 * g - 3)
                            else:
                                wait(dve, y_stored[p], 8 * (g - p) + 1)
                        dve.tensor_tensor(y[:, p, q // 2, q % 2 * HALF:q % 2 * HALF + HALF], p_m[:, q % 2, :],
                                          oscale[:, q % 2, :], ALU.mult).then_inc(m_scaled, 1)

                group_loop(dve, body)
                if X is not None:
                    out_stats(NG - 1, (NG - 1) % 2)
                    out_normalise(NG - 1, (NG - 1) % 2)

            @block.scalar
            def _(act):
                def copy_t(g, p, q):
                    act.wait_ge(t_full, 4 * g + q + 1)
                    wait(act, scaled, 8 * g - 16 + 2 * q + 2)
                    bank = p_n if early(g) and q % 2 else p_t
                    act.copy(xT[:, p, 2 * q:2 * q + 2, :], bank[:].rearrange("p (k t) -> p k t", k=2)).then_inc(t_copied, 1)

                def copy_logits(g):
                    act.wait_ge(l_full, g + 1)
                    act.copy(logT[:], p_r[0:E, 0:FTOK]).then_inc(l_copied, 1)

                def exponent(g):
                    act.wait_ge(sm_step, 6 * g + 2)
                    act.activation(r_exp[:], r_exp[:], ACT.Exp).then_inc(sm_exp, 1)

                def copy_routing(g, p):
                    act.wait_ge(r_full, g + 1)
                    act.copy(rT[:, p, :], p_r[:, 0:FTOK]).then_inc(r_copied, 1)

                def high(g, p, k):
                    act.wait_ge(scaled, 8 * g + k + 1)
                    wait(act, m_full, 4 * g - 4)
                    act.copy(a_hi[:, p, k, :], a_f[:, k % 2, :]).then_inc(hi_done, 1)

                def sign_w(k):
                    act.wait_ge(w_loaded[k % 4], 16 * (k // 4 + 1))
                    act.activation(wsign[:, k, :], w_raw[:, (k % 4) // 2, k % 2, :], ACT.Sign).then_inc(w_signed, 1)

                def copy_normed(g, c):
                    act.wait_ge(n_full, 4 * g + c + 2)
                    k0 = c % 2 * 4
                    bank = p_t if late(g) and c % 2 else p_n
                    act.copy(X[:, k0:k0 + 4, bass.ds(g * FTOK + (c // 2 * P + 1), P)],
                             bank[:].rearrange("p (k t) -> p k t", k=4)).then_inc(n_copied, 1)

                for q in range(4):
                    copy_t(0, 0, q)
                sign_w(0)
                sign_w(1)
                copy_logits(0)
                for q in range(4):
                    copy_t(1, 1, q)
                sign_w(2)
                exponent(0)
                sign_w(3)
                copy_routing(0, 0)
                for k in range(KD):
                    high(0, 0, k)
                copy_logits(1)
                for k in range(4, KD):
                    sign_w(k)
                exponent(1)
                for q in range(4):
                    copy_t(2, 0, q)

                def body(g, p):
                    for q in range(4):
                        act.wait_ge(o_full, 4 * g + q + 1)
                        wait(act, m_scaled, 4 * g + q - 1)
                        act.mul(oscale[:, q % 2, :], p_o[:], 0.5).then_inc(o_copied, 1)
                        if first_round(g) and q == 0:
                            copy_routing(1, 1)
                        if q == 3 and exists(g + 2):
                            copy_routing(g + 2, p)
                        if q == 0 and exists(g + 2):
                            copy_logits(g + 2)
                        if exists(g + 1):
                            high(g + 1, 1 - p, 2 * q)
                        if q == 3 and X is not None and exists(g - 1):
                            copy_normed(g - 1, 0)
                            copy_normed(g - 1, 1)
                        if exists(g + 1):
                            high(g + 1, 1 - p, 2 * q + 1)
                        if q == 3 and X is not None and exists(g - 1):
                            copy_normed(g - 1, 2)
                            copy_normed(g - 1, 3)
                        if q == 1 and exists(g + 2):
                            exponent(g + 2)
                        if exists(g + 3):
                            for piece in PIECES[q]:
                                copy_t(g + 3, 1 - p, piece)

                group_loop(act, body)
                if X is not None:
                    for c in range(4):
                        copy_normed(NG - 1, c)

            @block.tensor
            def _(pe):
                def transposes(g, p, q):
                    pe.wait_ge(x_normed, g + 1)
                    two = early(g)
                    wait(pe, t_copied, 4 * g + q - two)
                    bank = p_n if two and q % 2 else p_t
                    for c in range(2):
                        for t in range(FT):
                            k = 2 * q + c
                            last = pe.transpose(bank[:, c * FTOK + t * P:c * FTOK + t * P + P],
                                                xin[:, p, t, k * P:k * P + P], ident[:])
                    last.then_inc(t_full, 1)

                def logits(g, p, k0=0, k1=KD):
                    if k0 == 0:
                        pe.wait_ge(t_copied, 4 * g + 4)
                        wait(pe, r_copied, g)
                    for k in range(k0, k1):
                        last = pe.matmul(p_r[0:E, 0:FTOK], gateT[:, k, :], xT[:, p, k, :], start=(k == 0), stop=(k == KD - 1))
                    if k1 == KD:
                        last.then_inc(l_full, 1)

                def logits_back(g):
                    pe.wait_ge(l_copied, g + 1)
                    for t in range(FT):
                        last = pe.matmul(p_r[:, t * E:t * E + E], logT[:, t * P:t * P + P], ident[0:E, 0:E], start=True, stop=True)
                    last.then_inc(lt_full, 1)

                def routing(g):
                    pe.wait_ge(routing_ready, g + 1)
                    for t in range(FT):
                        last = pe.transpose(p_r[:, t * P:t * P + P], rt4[:, t, :], ident[:])
                    last.then_inc(r_full, 1)

                def in_scale(g, p, k):
                    pe.wait_ge(r_copied, g + 1)
                    wait(pe, scaled, 8 * g + k - 1)
                    pe.matmul(p_s[:, k % 2, 0:FTOK], ics3[:, k * P:k * P + P], rT[:, p, :],
                              start=True, stop=True).then_inc(s_full, 1)

                def out_scale(g, p, q):
                    wait(pe, o_copied, 4 * g + q)
                    pe.matmul(p_o[:], rT[:, p, q // 2 * P:q // 2 * P + P], ocs3[:, q % 2 * HALF:q % 2 * HALF + HALF],
                              start=True, stop=True).then_inc(o_full, 1)

                def product(g, p, q, k0, k1):
                    if k0 == 0:
                        wait(pe, m_scaled, 4 * g + q - 1)
                    for k in range(k0, k1):
                        if q == 0:
                            pe.wait_ge(w_signed, k + 1)
                            pe.wait_ge(lo_done, 8 * g + k + 1)
                        for part in (a_hi, a_lo):
                            last = pe.matmul(p_m[:, q % 2, :], part[:, p, k, q // 2 * P:q // 2 * P + P],
                                             wsign[:, k, q % 2 * HALF:q % 2 * HALF + HALF],
                                             start=(k == 0 and part is a_hi), stop=(k == KD - 1 and part is a_lo))
                    if k1 == KD:
                        last.then_inc(m_full, 1)

                def normed(g, p, c):
                    pe.wait_ge(y_normed, g + 2)
                    wait(pe, n_copied, 4 * g + c + 1 - (late(g) and c > 0))
                    if late(g):
                        pe.wait_ge(t_copied, 4 * NG)
                    bank = p_t if late(g) and c % 2 else p_n
                    for j in range(4):
                        k = c % 2 * 4 + j
                        last = pe.transpose(bank[:, j * P:j * P + P], y[:, p, c // 2, k * P:k * P + P], ident[:])
                    last.then_inc(n_full, 1)

                for q in range(4):
                    transposes(0, 0, q)
                pe.wait_ge(gate_loaded, 16)
                logits(0, 0)
                for q in range(4):
                    transposes(1, 1, q)
                    if q == 0:
                        logits_back(0)
                routing(0)
                pe.wait_ge(scales_split, 6)
                for k in range(KD):
                    in_scale(0, 0, k)
                    logits(1, 1, k, k + 1)
                logits_back(1)

                def body(g, p):
                    for q in range(4):
                        out_scale(g, p, q)
                        first = first_round(g) and q == 0
                        if first:
                            product(g, p, q, 0, 4)
                            for piece in range(4):
                                transposes(2, 0, piece)
                                product(g, p, q, piece + 4, piece + 5)
                            routing(1)
                        if exists(g + 1):
                            in_scale(g + 1, 1 - p, 2 * q)
                        if q == 3 and exists(g + 2):
                            routing(g + 2)
                        if q == 0 and exists(g + 2):
                            logits(g + 2, p)
                        if q == 3 and X is not None and exists(g - 1):
                            for c in range(4):
                                normed(g - 1, 1 - p, c)
                                product(g, p, q, 2 * c, 2 * c + 2)
                                if c == 1 and exists(g + 1):
                                    in_scale(g + 1, 1 - p, 2 * q + 1)
                                if c == 1 and exists(g + 3):
                                    transposes(g + 3, 1 - p, 2)
                        else:
                            if not first:
                                product(g, p, q, 0, 4)
                            if exists(g + 1):
                                in_scale(g + 1, 1 - p, 2 * q + 1)
                            if q == 3 and exists(g + 3):
                                transposes(g + 3, 1 - p, 2)
                            if q == 0 and exists(g + 2):
                                logits_back(g + 2)
                            if not first:
                                product(g, p, q, 4, KD)
                        if q and exists(g + 3):
                            transposes(g + 3, 1 - p, (0, 1, 3)[q - 1])

                group_loop(pe, body)
                if X is not None:
                    for c in range(4):
                        normed(NG - 1, (NG - 1) % 2, c)


PAIRS = T // 2
NB = PAIRS // HALF
FILTERS = [
    (-1, 1, ALU.subtract, (0,)),
    (0, 1, ALU.add, (0, 1, 2)),
    (1, 0, ALU.subtract, (0, 1, 2)),
    (0, 2, ALU.subtract, (2,)),
]
NF = len(FILTERS)
KQ = KD // 2


def conv_phase(nc, sems, conv_w, conv_b, Yd, X, attention_weights, x_room):
    def sem(name):
        return sems.enter_context(nc.semaphore(f"c_{name}"))

    bias_loaded = sem("bias_loaded")
    raw_loaded = [sem(f"raw_loaded{h}") for h in range(2)]
    outer_summed, tap_ready, g_hi, g_lo = sem("outer_summed"), sem("tap_ready"), sem("g_hi"), sem("g_lo")
    d_pool, d_dve, d_hi, d_lo = sem("d_pool"), sem("d_dve"), sem("d_hi"), sem("d_lo")
    chunk_used, m_added, y_stored = sem("chunk_used"), sem("m_added"), sem("y_stored")
    w_loaded, w_hi, w_lo = sem("w_loaded"), sem("w_hi"), sem("w_lo")

    with ExitStack() as ctx:
        def sb(name, shape, dt=F32):
            return ctx.enter_context(nc.sbuf_tensor(f"c_{name}", shape, dt))

        dhi = sb("dhi", [P, KD, PAIRS], F32R)
        dlo = sb("dlo", [P, KD, PAIRS], F32R)
        df = sb("df", [P, 2, NB, HALF])
        Y = sb("Y", [P, NCH, T])
        ghi = sb("ghi", [P, 2, KQ * P], F32R)
        glo = sb("glo", [P, 2, KQ * P], F32R)
        raw = sb("raw", [P, 2, TAPS, KQ * P])
        cb = sb("cb", [P, NCH])
        p_m = ctx.enter_context(nc.psum_tensor("c_p_m", [P, 2, NB, HALF], F32))
        w_parts = [(X[:, 2 * n + 1, 0:w.shape[1]], x_room[:, 2 * n, 0:w.shape[1]], x_room[:, 2 * n + 1, 0:w.shape[1]])
                   for n, w in enumerate(attention_weights)]
        Yp = Y[:].rearrange("p c (n e) -> p c n e", e=2)

        with nc.Block() as block:

            def pooled(n, b):
                return n // 2 * 3 + n % 2 + b + 1

            @block.sync
            def _(sp):
                def load(j, c, h):
                    taps = FILTERS[j][3]
                    sp.dma_start(raw[:, h, taps[0]:taps[-1] + 1, :], conv_w[c, h, :, taps[0]:taps[-1] + 1, :]).then_inc(raw_loaded[h], 16)

                sp.dma_start(cb[:], conv_b).then_inc(bias_loaded, 16)
                for j in range(NF):
                    def body(c):
                        for h in range(2):
                            wait(sp, g_lo, (j * NCH + c) * 2 + h - 1)
                            load(j, c, h)

                    body(0)
                    body(1)
                    if j == NF - 1:
                        for n, w in enumerate(attention_weights):
                            sp.wait_ge(d_pool, pooled(j * KD + 2 * n + 1, 1))
                            sp.wait_ge(d_dve, (j * KD + 2 * n) // 2 + 1)
                            sp.dma_start(w_parts[n][0], w).then_inc(w_loaded, 16)
                    with sp.Fori(2, NCH) as c:
                        body(c)
                for c in range(NCH):
                    sp.wait_ge(m_added, (NF - 1) * NCH + c + 1)
                    sp.dma_start(Yd[c], Y[:, c, :]).then_inc(y_stored, 16)
                sp.wait_ge(y_stored, 16 * NCH)

            def pair_values(k, b, token):
                start = 2 * b * HALF + token + 1
                return X[:, k, start:start + 2 * HALF - 1:2]

            @block.gpsimd
            def _(pool):
                for j, (one, other, op, _) in enumerate(FILTERS):
                    for k in range(KD):
                        n = j * KD + k
                        wait(pool, d_hi, 2 * n - 2)
                        wait(pool, d_lo, 2 * n - 2)
                        for b in range(NB if k % 2 else 1):
                            if op == ALU.add:
                                made = pool.tensor_tensor(df[:, k % 2, b, :], pair_values(k, b, one), pair_values(k, b, other), ALU.add)
                            else:
                                made = pool.tensor_tensor(df[:, k % 2, b, :], pair_values(k, b, one), pair_values(k, b, other), ALU.subtract)
                            made.then_inc(d_pool, 1)

            @block.scalar
            def _(act):
                def split_data(j, k):
                    n = j * KD + k
                    if j:
                        act.wait_ge(chunk_used, (j * NCH - 1) * KD + k + 1)
                    for b in range(NB):
                        if b and k % 2 == 0:
                            act.wait_ge(d_dve, n // 2 + 1)
                        else:
                            act.wait_ge(d_pool, pooled(n, b))
                        act.copy(dhi[:, k, b * HALF:b * HALF + HALF], df[:, k % 2, b, :]).then_inc(d_hi, 1)

                def split_filter(j, c, h):
                    n = (j * NCH + c) * 2 + h
                    taps = FILTERS[j][3]
                    if len(taps) == 1:
                        act.wait_ge(raw_loaded[h], 8 * (n - h) + 16)
                        source = raw[:, h, taps[0], :]
                    else:
                        act.wait_ge(tap_ready, n + 1 - 2 * NCH)
                        source = raw[:, h, 0, :]
                    wait(act, chunk_used, 4 * n - 4)
                    act.copy(ghi[:, h, :], source).then_inc(g_hi, 1)

                for j in range(NF):
                    for h in range(2):
                        split_filter(j, 0, h)
                        for k in range(KQ * h, KQ * h + KQ):
                            split_data(j, k)
                    if j < NF - 1:
                        with act.Fori(1, NCH) as c:
                            for h in range(2):
                                split_filter(j, c, h)
                    else:
                        for c in range(1, NCH):
                            for h in range(2):
                                split_filter(j, c, h)
                            if c >= 2:
                                act.wait_ge(w_loaded, 16 * len(w_parts))
                                act.copy(w_parts[c - 2][1], w_parts[c - 2][0]).then_inc(w_hi, 1)

            @block.vector
            def _(dve):
                def operand(j, k):
                    one, other, op, _ = FILTERS[j]
                    n = j * KD + k
                    wait(dve, d_hi, 2 * n - 2)
                    wait(dve, d_lo, 2 * n - 2)
                    dve.tensor_tensor(df[:, 0, 1, :], pair_values(k, 1, one), pair_values(k, 1, other), op).then_inc(d_dve, 1)

                def low_data(j, k):
                    n = j * KD + k
                    for b in range(NB):
                        dve.wait_ge(d_hi, 2 * n + b + 1)
                        cols = slice(b * HALF, b * HALF + HALF)
                        dve.tensor_tensor(dlo[:, k, cols], df[:, k % 2, b, :], dhi[:, k, cols].bitcast(F32), ALU.subtract).then_inc(d_lo, 1)

                def combine(j, c, h):
                    n = (j * NCH + c) * 2 + h
                    if len(FILTERS[j][3]) == TAPS:
                        m = n - 2 * NCH
                        dve.wait_ge(raw_loaded[h], 8 * (n - h) + 16)
                        dve.tensor_tensor(raw[:, h, 0, :], raw[:, h, 0, :], raw[:, h, 2, :], ALU.add).then_inc(outer_summed, 1)
                        dve.wait_ge(outer_summed, m + 1)
                        dve.tensor_tensor(raw[:, h, 0, :], raw[:, h, 0, :], raw[:, h, 1, :],
                                          ALU.add if j == 1 else ALU.subtract).then_inc(tap_ready, 1)

                def low_filter(j, c, h):
                    n = (j * NCH + c) * 2 + h
                    if len(FILTERS[j][3]) == TAPS:
                        dve.wait_ge(tap_ready, n - 2 * NCH + 1)
                    dve.wait_ge(g_hi, n + 1)
                    dve.tensor_tensor(glo[:, h, :], raw[:, h, FILTERS[j][3][0], :], ghi[:, h, :].bitcast(F32), ALU.subtract).then_inc(g_lo, 1)

                def add(j, c, p):
                    n = j * NCH + c
                    m = p_m[:, p]
                    even = Yp[:, bass.ds(c, 1), :, 0]
                    odd = Yp[:, bass.ds(c, 1), :, 1]
                    even, odd = (y.rearrange("p c (b n) -> p (c b) n", b=NB) for y in (even, odd))
                    bias = cb[:, bass.ds(c, 1)]
                    dve.wait_ge(chunk_used, 8 * n + 8)
                    if j:
                        dve.wait_ge(m_added, n - NCH + 1)
                    if j == 0:
                        dve.tensor_scalar(even, m, bias, None, ALU.add).then_inc(m_added, 1)
                    if j == 1:
                        dve.tensor_scalar(odd, m, 0.5, bias, ALU.mult, ALU.add)
                        dve.scalar_tensor_tensor(even, m, 0.5, even, ALU.mult, ALU.add).then_inc(m_added, 1)
                    if j == 2:
                        dve.scalar_tensor_tensor(odd, m, -0.5, odd, ALU.mult, ALU.add)
                        dve.scalar_tensor_tensor(even, m, 0.5, even, ALU.mult, ALU.add).then_inc(m_added, 1)
                    if j == 3:
                        dve.scalar_tensor_tensor(odd, m, -1.0, odd, ALU.mult, ALU.add).then_inc(m_added, 1)

                dve.wait_ge(bias_loaded, 16)
                for j in range(NF):
                    combine(j, 0, 0)
                    combine(j, 0, 1)
                    operand(j, 0)
                    low_filter(j, 0, 0)
                    for k in range(KD):
                        low_data(j, k)
                        if k % 2 and k < KD - 1:
                            operand(j, k + 1)
                        if k == KQ - 1:
                            low_filter(j, 0, 1)
                        if k == KD - 3 and j:
                            add(j - 1, NCH - 1, 1)
                    combine(j, 1, 0)
                    low_filter(j, 1, 0)
                    def body(c, p, last=False):
                        combine(j, c, 1)
                        low_filter(j, c, 1)
                        add(j, c - 1, 1 - p)
                        if not last:
                            combine(j, c + 1, 0)
                            low_filter(j, c + 1, 0)

                    if j < NF - 1:
                        with dve.Fori(0, (NCH - 1) // 2) as i:
                            body(2 * i + 1, 1)
                            body(2 * i + 2, 0)
                        body(NCH - 1, 1, last=True)
                    else:
                        for c in range(1, NCH):
                            body(c, c % 2, last=c == NCH - 1)
                            if c >= 2:
                                dve.wait_ge(w_hi, c - 1)
                                whole, high, low = w_parts[c - 2]
                                dve.tensor_tensor(low, whole, high.bitcast(F32), ALU.subtract).then_inc(w_lo, 1)
                add(NF - 1, NCH - 1, 1)

            @block.tensor
            def _(pe):
                def products(j, c, p):
                    n = j * NCH + c
                    wait(pe, m_added, n - 1)
                    for h in range(2):
                        pe.wait_ge(g_lo, 2 * n + h + 1)
                        for q in range(KQ):
                            k = KQ * h + q
                            pe.wait_ge(d_lo, 2 * (j * KD + k) + 2)
                            for w, parts in ((ghi, (dhi, dlo)), (glo, (dhi,))):
                                for b in range(NB):
                                    for part in parts:
                                        last = pe.matmul(p_m[:, p, b, :], w[:, h, q * P:q * P + P],
                                                         part[:, k, b * HALF:b * HALF + HALF],
                                                         start=(k == 0 and w is ghi and part is dhi), stop=(k == KD - 1 and w is glo))
                            last.then_inc(chunk_used, 1)

                for j in range(NF):
                    products(j, 0, 0)
                    products(j, 1, 1)
                    with pe.Fori(1, NCH // 2) as i:
                        products(j, 2 * i, 0)
                        products(j, 2 * i + 1, 1)


GT = 4
GTOK = GT * P
AG = T // GTOK
QUADS = H // 4
UNITS = QUADS * GT
SLOTS = 4
T_LAG, V_LAG = 3, 4
ROUNDS = UNITS + V_LAG
WEIGHTS = ("wq", "wk", "wv", "wo")


def general(first, last):
    rounds = [[] for _ in range(ROUNDS)]
    for u in range(4 * QUADS - 4):
        rounds[u].append(("qk", 0, u + 4))
    if not first:
        for n, u in enumerate((1, 3, 5, 7, 9, 11, 12, 13)):
            rounds[u].append(("proj", -1, n))
    after = [("wo", 0, m) for m in range(WC)]
    if not last:
        for n, part in enumerate((0, 2, 1, 3)):
            rounds[14 + n].append(("qk", 1, part))
        rounds[19].append(("v", 1, 0))
        after = [("v", 1, n) for n in range(1, 2 * GT)] + after
    return rounds, after


BEFORE = [("qk", 0, part) for part in range(4)] + [("v", 0, n) for n in range(2 * GT)]
AFTER = [("proj", 0, n) for n in range(2 * GT)]
TAKES_FIRST = (0, 2, 4, 6, 8, 10, 14, 15)
SPLIT_ROUNDS = (11, 11, 13, 14, 17, 17)


def flat(first, last):
    rounds, after = general(first, last)
    return sum(rounds, []) + after


def number(g, first, last, step):
    start = len(BEFORE) if first else len(BEFORE) + len(flat(True, False)) + len(flat(False, False)) * (g - 1)
    return start + flat(first, last).index(step)


def attention_phase(nc, sems, Yd, x1, x2, x_room, wp, bq, bk, bv, bo, bp, ident):
    def sem(name):
        return sems.enter_context(nc.semaphore(f"a_{name}"))

    wp_loaded, bias_loaded, q_zeroed, mask_made = sem("wp_loaded"), sem("bias_loaded"), sem("q_zeroed"), sem("mask_made")
    wp_hi, wp_lo = sem("wp_hi"), sem("wp_lo")
    y_loaded = [sem(f"y_loaded{s}") for s in range(2)]
    xs_hi, xs_lo = sem("xs_hi"), sem("xs_lo")
    gen_full = sem("gen_full")
    q_ready, k_ready, v_ready = sem("q_ready"), sem("k_ready"), sem("v_ready")
    s_full, s_masked, s_max, s_bias, exp_done = sem("s_full"), sem("s_masked"), sem("s_max"), sem("s_bias"), sem("exp_done")
    sum_inverted, probs_ready = sem("sum_inverted"), sem("probs_ready")
    pt_full, pt_copied, pv_done = sem("pt_full"), sem("pt_copied"), sem("pv_done")
    o_hi, o_lo = sem("o_hi"), sem("o_lo")
    oo_hi, oo_lo = sem("oo_hi"), sem("oo_lo")
    x_loaded, x_biased, x_summed, x_stored = ([sem(f"{n}{t}") for t in range(GT)] for n in ("x_loaded", "x_biased", "x_summed", "x_stored"))

    x1v = x1.rearrange("(g t p) d -> g t p d", p=P, t=GT)
    x2v = x2.rearrange("(g t p) d -> g t p d", p=P, t=GT)

    with ExitStack() as ctx:
        def sb(name, shape, dt=F32):
            return ctx.enter_context(nc.sbuf_tensor(f"a_{name}", shape, dt))

        def ps(name, shape):
            return ctx.enter_context(nc.psum_tensor(f"a_{name}", shape, F32))

        hi, lo = {}, {}
        for n, name in enumerate(WEIGHTS):
            for part, w in enumerate((hi, lo)):
                w[name] = x_room[:, 2 * n + part, 0:WC * HE].rearrange("p (c n) -> p c n", c=KH if name == "wo" else WC)
        hi["wp"] = sb("wp_hi", [P, WC, D], F32R)
        wp_at = nc.sbuf_base
        wp_raw = sb("wp_raw", [P, WC, D])
        lo["wp"] = nc.alloc_sbuf_tensor_at("a_wp_lo", [P, WC, D], F32R, offset=wp_at)
        xs = [sb(f"xs_{n}", [P, NCH, GTOK], F32R) for n in ("hi", "lo")]
        oo = [x[:, 2 * WC:NCH, :] for x in xs]
        yc = sb("yc", [P, 2, GTOK])
        q = sb("q", [P, 2, 2, 2, GTOK])
        kk = sb("kk", [P, 2, 2, GTOK])
        v = sb("v", [P, GT, HE])
        start_cells = sb("start_cells", [P, 2])
        residual = sb("residual", [P, 2, D])
        s = sb("s", [P, SLOTS, 4, P])
        nmx = sb("nmx", [P, SLOTS, 4])
        sums = sb("sums", [P, SLOTS, 4])
        pt = sb("pt", [P, 2, 4, P])
        oT = [sb(f"oT_{n}", [P, KH, GTOK], F32R) for n in ("hi", "lo")]
        bqs, bks, bvs, bos = sb("bqs", [P, KH]), sb("bks", [P, KH]), sb("bvs", [P, KH]), sb("bos", [P, WC])
        bps = sb("bps", [P, D])
        mask = sb("mask", [P, P])
        p_s, p_t, p_g = ps("p_s", [P, 2, HALF]), ps("p_t", [P, 2, HALF]), ps("p_g", [P, 2, HALF])
        p_o = ps("p_o", [P, 2, HALF])

        def place(g, t):
            n, before = (t, 0 if t >= 2 else 2 * g) if isinstance(g, int) and g == AG - 1 else (t % 2, 2 * g + t // 2)
            return n, residual[:, n, :] if n < 2 else v[:, n, :], before

        def parts(tensors):
            (lh, ll), (rh, rl) = tensors
            return ((lh, rh), (lh, rl), (ll, rh))

        def groups(eng, body):
            body(0, True, False)
            with eng.Fori(1, AG - 1) as g:
                body(g, False, False)
            body(AG - 1, False, True)

        with nc.Block() as block:

            @block.sync
            def _(sp):
                def load_y(g, c):
                    wait(sp, xs_lo, NCH * g + c - 1)
                    sp.dma_start(yc[:, c % 2, :], Yd[c, :, bass.ds(g * GTOK, GTOK)]).then_inc(y_loaded[c % 2], 16)

                def load_x(g, t):
                    n, room, before = place(g, t)
                    if n < 2:
                        sp.wait_ge(x_stored[n], 16 * before + 1)
                    sp.dma_start(room, x1v[g, t]).then_inc(x_loaded[n], 16)

                def store_x(g, t):
                    n, room, before = place(g, t)
                    sp.wait_ge(x_summed[n], 2 * before + 2)
                    sp.dma_start(x2v[g, t], room).then_inc(x_stored[n], 16)

                load_y(0, 0)
                load_y(0, 1)
                for to, of in ((bqs, bq), (bks, bk)):
                    sp.dma_start(to[:], of).then_inc(bias_loaded, 16)
                for c in range(2, NCH):
                    load_y(0, c)
                for to, of in ((bvs, bv), (bos, bo), (bps, bp.partition_broadcast(P))):
                    sp.dma_start(to[:], of).then_inc(bias_loaded, 16)
                sp.dma_start(wp_raw[:], wp).then_inc(wp_loaded, 16)

                def body(g, first, last):
                    if not last:
                        load_y(g + 1, 0)
                        load_y(g + 1, 1)
                    if not first:
                        load_x(g - 1, 0)
                        load_x(g - 1, 1)
                        store_x(g - 1, 0)
                        load_x(g - 1, 2)
                        store_x(g - 1, 1)
                        load_x(g - 1, 3)
                        store_x(g - 1, 2)
                    if not last:
                        load_y(g + 1, 2)
                        load_y(g + 1, 3)
                    if not first:
                        store_x(g - 1, 3)
                    if not last:
                        load_y(g + 1, 4)
                        load_y(g + 1, 5)

                groups(sp, body)
                load_x(AG - 1, 0)
                load_x(AG - 1, 1)
                sp.wait_ge(pv_done, UNITS * AG)
                load_x(AG - 1, 2)
                load_x(AG - 1, 3)
                for t in range(GT):
                    store_x(AG - 1, t)
                for t in range(GT):
                    n, _, before = place(AG - 1, t)
                    sp.wait_ge(x_stored[n], 16 * (before + 1) + (n < 2))

            @block.gpsimd
            def _(pool):
                pool.memset(q[:, 0], 0.0).then_inc(q_zeroed, 1)
                pool.memset(mask[:], 0.0).then_inc(mask_made, 1)
                pool.wait_ge(mask_made, 1)
                pool.affine_select(out=mask[:], in_=mask[:], compare_op=ALU.is_ge, fill=MASKED, base=0,
                                   pattern=[[-1, P]], channel_multiplier=1).then_inc(mask_made, 1)
                pool.memset(q[:, 1], 0.0).then_inc(q_zeroed, 1)
                pool.wait_ge(bias_loaded, 5 * 16)

                def add_bias(g, t):
                    n, room, before = place(g, t)
                    pool.wait_ge(x_loaded[n], 16 * before + 16)
                    pool.tensor_tensor(room, room, bps[:], ALU.add).then_inc(x_biased[n], 1)

                def body(g, first, last):
                    if not first:
                        add_bias(g - 1, 0)
                        add_bias(g - 1, 1)
                    for u in range(UNITS):
                        pool.wait_ge(sum_inverted, UNITS * g + u + 1)
                        r = u % SLOTS
                        pool.tensor_tensor(s[:, r], s[:, r], sums[:, r].unsqueeze(2).broadcast_to([P, 4, P]),
                                           ALU.mult).then_inc(probs_ready, 1)
                        if not first and u in (5, 9):
                            add_bias(g - 1, (5, 9).index(u) + 2)

                groups(pool, body)
                for t in range(GT):
                    add_bias(AG - 1, t)

            @block.scalar
            def _(act):
                def split_high(g, c):
                    act.wait_ge(y_loaded[c % 2], 48 * g + 16 * (c // 2) + 16)
                    act.copy(xs[0][:, c, :], yc[:, c % 2, :]).then_inc(xs_hi, 1)

                def take(g, count, bank, step):
                    what, offset, i = step
                    p = p_g[:, bank, :]
                    if what == "qk" and i % 2 == 0:
                        act.wait_ge(gen_full, count)
                        wait(act, s_full, UNITS * (g + offset) + 4 * (i // 4) - 4)
                        c = i // 2
                        for head in range(2):
                            rows = slice(DH * head, DH * head + DH)
                            done = act.activation(q[rows, c // 2 % 2, c % 2, head, :], p[rows, :], ACT.Identity, bias=bqs[rows, c:c + 1])
                        done.then_inc(q_ready, 1)
                    if what == "v":
                        act.wait_ge(gen_full, count)
                        wait(act, pv_done, UNITS * (g + offset))
                        act.copy(v[:, i // 2, i % 2 * HALF:i % 2 * HALF + HALF], p).then_inc(v_ready, 1)
                    if what == "wo":
                        act.wait_ge(gen_full, count)
                        act.activation(oo[0][:, i, :], p, ACT.Identity, bias=bos[:, i:i + 1]).then_inc(oo_hi, 1)

                for c in range(2 * WC):
                    split_high(0, c)
                act.wait_ge(bias_loaded, 2 * 16)
                act.wait_ge(q_zeroed, 1)
                for n, step in enumerate(BEFORE):
                    if n % 4 == 0 and n < 4 * WC:
                        split_high(0, 2 * WC + n // 4)
                    take(0, n + 1, n % 2, step)
                act.wait_ge(bias_loaded, 5 * 16)
                act.wait_ge(q_zeroed, 2)
                act.wait_ge(wp_loaded, 16)
                act.copy(hi["wp"][:], wp_raw[:]).then_inc(wp_hi, 1)

                def body(g, first, last):
                    rounds, after = general(first, last)
                    for u in range(ROUNDS):
                        if u in TAKES_FIRST:
                            for step in rounds[u]:
                                n = number(g, first, last, step)
                                take(g, n + 1, flat(first, last).index(step) % 2, step)
                        if u < UNITS:
                            act.wait_ge(s_bias, UNITS * g + u + 1)
                            r = u % SLOTS
                            for h in range(4):
                                done = act.activation(s[:, r, h, :], s[:, r, h, :], ACT.Exp, bias=nmx[:, r, h:h + 1],
                                                      scale=SCALE, accum_out=sums[:, r, h:h + 1])
                            done.then_inc(exp_done, 1)
                        if u not in TAKES_FIRST:
                            for step in rounds[u]:
                                n = number(g, first, last, step)
                                take(g, n + 1, flat(first, last).index(step) % 2, step)
                        for c in range(NCH):
                            if not last and u == SPLIT_ROUNDS[c]:
                                reader = ("qk", 0, 4 * QUADS - 2 + c // 2) if c < 2 * WC else ("proj", -1, 2 * GT - 1)
                                if reader in flat(first, last):
                                    act.wait_ge(gen_full, number(g, first, last, reader) + 1)
                                split_high(g + 1, c)
                        if u >= V_LAG + 3 and (u - V_LAG - 3) % 4 == 0:
                            quad = (u - V_LAG - 3) // 4
                            act.wait_ge(pv_done, UNITS * g + 4 * quad + 4)
                            if not first:
                                act.wait_ge(gen_full, number(g, first, last, rounds[0][0]))
                            for i in range(2):
                                act.activation(oT[0][:, 2 * quad + i, :], p_o[:, i, :], ACT.Identity,
                                               bias=bvs[:, 2 * quad + i:2 * quad + i + 1]).then_inc(o_hi, 1)
                    for step in after:
                        n = number(g, first, last, step)
                        take(g, n + 1, flat(first, last).index(step) % 2, step)

                groups(act, body)

            @block.vector
            def _(dve):
                for n in range(2):
                    dve.memset(start_cells[:, n:n + 1], 0.0).then_inc(x_stored[n], 1)

                def split_low(g, c):
                    dve.wait_ge(xs_hi, NCH * g + c + 1)
                    dve.tensor_tensor(xs[1][:, c, :], yc[:, c % 2, :], xs[0][:, c, :].bitcast(F32), ALU.subtract).then_inc(xs_lo, 1)

                def take(g, count, bank, step):
                    what, offset, i = step
                    p = p_g[:, bank, :]
                    if what == "qk" and i % 2 == 1:
                        dve.wait_ge(gen_full, count)
                        wait(dve, s_full, UNITS * (g + offset) + 4 * (i // 4) - 4)
                        c = i // 2
                        dve.tensor_scalar(kk[:, c // 2 % 2, c % 2, :], p, bks[:, c:c + 1], None, ALU.add).then_inc(k_ready, 1)
                    if what == "wo":
                        dve.wait_ge(oo_hi, WC * (g + offset) + i + 1)
                        dve.scalar_tensor_tensor(oo[1][:, i, :], p, bos[:, i:i + 1], oo[0][:, i, :].bitcast(F32),
                                                 ALU.add, ALU.subtract).then_inc(oo_lo, 1)
                    if what == "proj":
                        n, room, before = place(g + offset, i // 2)
                        dve.wait_ge(gen_full, count)
                        dve.wait_ge(x_biased[n], before + 1)
                        cols = room[:, i % 2 * HALF:i % 2 * HALF + HALF]
                        dve.tensor_tensor(cols, p, cols, ALU.add).then_inc(x_summed[n], 1)

                for c in range(2 * WC):
                    split_low(0, c)
                dve.wait_ge(bias_loaded, 2 * 16)
                for n, step in enumerate(BEFORE):
                    if n % 4 == 0 and n < 4 * WC:
                        split_low(0, 2 * WC + n // 4)
                    take(0, n + 1, n % 2, step)
                dve.wait_ge(bias_loaded, 5 * 16)
                dve.wait_ge(mask_made, 2)

                def body(g, first, last):
                    rounds, after = general(first, last)
                    for u in range(ROUNDS):
                        if u < UNITS:
                            n, r = UNITS * g + u, u % SLOTS
                            dve.wait_ge(s_full, n + 1)
                            wait(dve, pt_full, n - SLOTS + 1)
                            dve.tensor_tensor(s[:, r], p_s[:, u % 2, :].rearrange("p (h t) -> p h t", h=4),
                                              mask[:].unsqueeze(1).broadcast_to([P, 4, P]), ALU.add).then_inc(s_masked, 1)
                            dve.wait_ge(s_masked, n + 1)
                            dve.tensor_reduce(sums[:, r], s[:, r], AX.X, ALU.max).then_inc(s_max, 1)
                            dve.wait_ge(s_max, n + 1)
                            dve.tensor_scalar(nmx[:, r], sums[:, r], -SCALE, None, ALU.mult).then_inc(s_bias, 1)
                        if 1 <= u <= UNITS:
                            n, r = UNITS * g + u - 1, (u - 1) % SLOTS
                            dve.wait_ge(exp_done, n + 1)
                            dve.reciprocal(sums[:, r], sums[:, r]).then_inc(sum_inverted, 1)
                        for step in rounds[u]:
                            n = number(g, first, last, step)
                            take(g, n + 1, flat(first, last).index(step) % 2, step)
                        if T_LAG <= u < UNITS + T_LAG:
                            n, slot = UNITS * g + u - T_LAG, (u - T_LAG) % 2
                            dve.wait_ge(pt_full, n + 1)
                            wait(dve, pv_done, n - 1)
                            dve.tensor_copy(pt[:, slot].rearrange("p h t -> p (h t)"), p_t[:, slot, :]).then_inc(pt_copied, 1)
                        for c in range(NCH):
                            if not last and u == SPLIT_ROUNDS[c] + 1:
                                split_low(g + 1, c)
                        if u >= V_LAG + 3 and (u - V_LAG - 3) % 4 == 0:
                            quad = (u - V_LAG - 3) // 4
                            for i in range(2):
                                c = 2 * quad + i
                                dve.wait_ge(o_hi, KH * g + c + 1)
                                dve.scalar_tensor_tensor(oT[1][:, c, :], p_o[:, i, :], bvs[:, c:c + 1], oT[0][:, c, :].bitcast(F32),
                                                         ALU.add, ALU.subtract).then_inc(o_lo, 1)
                    if first:
                        dve.wait_ge(wp_hi, 1)
                        dve.tensor_tensor(lo["wp"][:], wp_raw[:], hi["wp"][:].bitcast(F32), ALU.subtract).then_inc(wp_lo, 1)
                    for step in after:
                        n = number(g, first, last, step)
                        take(g, n + 1, flat(first, last).index(step) % 2, step)

                groups(dve, body)
                for n, step in enumerate(AFTER):
                    take(AG - 1, number(AG - 1, False, True, ("wo", 0, WC - 1)) + n + 2, n % 2, step)

            @block.tensor
            def _(pe):
                def bank_taken(g, step):
                    what, offset, i = step
                    g = g + offset
                    if what == "qk":
                        wait(pe, k_ready if i % 2 else q_ready, 2 * QUADS * g + i // 2 + 1)
                    if what == "v":
                        wait(pe, v_ready, 2 * GT * g + i + 1)
                    if what == "wo":
                        wait(pe, oo_lo, WC * g + i + 1)
                    if what == "proj":
                        n, _, before = place(g, i // 2)
                        wait(pe, x_summed[n], 2 * before + i % 2 + 1)

                def product(g, bank, step):
                    what, offset, i = step
                    g = g + offset
                    if what == "qk":
                        pe.wait_ge(xs_lo, NCH * g + (i % 2 + 1) * WC)
                        name, c0, out = ("wq", "wk")[i % 2], i % 2 * WC, slice(i // 2 * P, i // 2 * P + P)
                        pairs = [(a[:, c, out], b[:, c0 + c, :]) for c in range(WC) for a, b in parts(((hi[name], lo[name]), xs))]
                    if what == "v":
                        pe.wait_ge(xs_lo, NCH * g + NCH)
                        tokens, cols = slice(i // 2 * P, i // 2 * P + P), slice(i % 2 * HALF, i % 2 * HALF + HALF)
                        pairs = [(a[:, 2 * WC + c, tokens], b[:, c, cols]) for c in range(WC) for a, b in parts((xs, (hi["wv"], lo["wv"])))]
                    if what == "wo":
                        out = slice(i * P, i * P + P)
                        pairs = [(a[:, c, out], b[:, c, :]) for c in range(KH) for a, b in parts(((hi["wo"], lo["wo"]), oT))]
                    if what == "proj":
                        pe.wait_ge(oo_lo, WC * g + WC)
                        tokens, cols = slice(i // 2 * P, i // 2 * P + P), slice(i % 2 * HALF, i % 2 * HALF + HALF)
                        pairs = [(a[:, c, tokens], b[:, c, cols]) for c in range(WC) for a, b in parts((oo, (hi["wp"], lo["wp"])))]
                    for n, (a, b) in enumerate(pairs):
                        if what == "wo" and n % 3 == 0:
                            pe.wait_ge(o_lo, KH * g + n // 3 + 1)
                        mm = pe.matmul(p_g[:, bank, :], a, b, start=n == 0, stop=n == len(pairs) - 1)
                    mm.then_inc(gen_full, 1)

                def body(g, first, last):
                    rounds, after = general(first, last)
                    steps = flat(first, last)
                    two_before = (BEFORE[-2:] if first else [("wo", -1, m) for m in range(WC)]) + steps

                    def general_product(step):
                        n = steps.index(step)
                        bank_taken(g, two_before[n])
                        product(g, n % 2, step)

                    for u in range(ROUNDS):
                        if u < UNITS:
                            quad, t = u // GT, u % GT
                            if t == 0:
                                pe.wait_ge(q_ready, 2 * QUADS * g + 2 * quad + 2)
                                pe.wait_ge(k_ready, 2 * QUADS * g + 2 * quad + 2)
                            wait(pe, s_masked, UNITS * g + u - 1)
                            for h in range(4):
                                mm = pe.matmul(p_s[:, u % 2, h * P:h * P + P], q[:, quad % 2, h // 2, h % 2, t * P:t * P + P],
                                               kk[:, quad % 2, h // 2, t * P:t * P + P], start=True, stop=True)
                            mm.then_inc(s_full, 1)
                        for step in rounds[u]:
                            general_product(step)
                        if T_LAG <= u < UNITS + T_LAG:
                            w = u - T_LAG
                            pe.wait_ge(probs_ready, UNITS * g + w + 1)
                            wait(pe, pt_copied, UNITS * g + w - 1)
                            for h in range(4):
                                mm = pe.transpose(p_t[:, w % 2, h * P:h * P + P], s[:, w % SLOTS, h, :], ident[:])
                            mm.then_inc(pt_full, 1)
                        if u >= V_LAG:
                            w = u - V_LAG
                            quad, t = w // GT, w % GT
                            pe.wait_ge(pt_copied, UNITS * g + w + 1)
                            if w == 0:
                                pe.wait_ge(v_ready, 2 * GT * g + 2 * GT)
                            if t == 0:
                                wait(pe, o_lo, KH * g + 2 * quad)
                            for h in range(4):
                                head = 4 * quad + h
                                mm = pe.matmul(p_o[DH * (h % 2):DH * (h % 2) + DH, h // 2, t * P:t * P + P],
                                               v[:, t, head * DH:head * DH + DH], pt[:, w % 2, h, :], start=True, stop=True)
                            mm.then_inc(pv_done, 1)
                    for step in after:
                        general_product(step)

                for n, step in enumerate(BEFORE):
                    if n >= 2:
                        bank_taken(0, BEFORE[n - 2])
                    product(0, n % 2, step)
                groups(pe, body)
                pe.wait_ge(wp_lo, 1)
                two_before = [("wo", 0, m) for m in range(WC)] + AFTER
                for n, step in enumerate(AFTER):
                    bank_taken(AG - 1, two_before[n])
                    product(AG - 1, n % 2, step)


def macaron_kernel(nc, x, conv_w, conv_b, wq, bq, wk, bk, wv, bv, wo, bo, wp, bp, w_t, bias, gate_t, ics, ocs, out):
    x1 = nc.dram_tensor("x_after_ffn1", (T, D), F32).ap()
    x2 = nc.dram_tensor("x_after_attention", (T, D), F32).ap()
    conv_out = nc.dram_tensor("conv_out", (NCH, P, T), F32).ap()

    with ExitStack() as sems, ExitStack() as ctx:
        ident = ctx.enter_context(nc.sbuf_tensor("ident", [P, P], F32))
        zeroed = sems.enter_context(nc.semaphore("zeroed"))

        with nc.Block() as block:
            @block.gpsimd
            def _(pool):
                pool.memset(ident[:], 0.0).then_inc(zeroed, 1)
                pool.wait_ge(zeroed, 1)
                pool.affine_select(out=ident[:], in_=ident[:], compare_op=ALU.not_equal, fill=1.0, base=0,
                                   pattern=[[-1, P]], channel_multiplier=1)

        x_at = nc.sbuf_base
        with nc.sbuf_tensor("X", [P, KD, T + 2], F32) as X:
            x_room = nc.alloc_sbuf_tensor_at("x_room", [P, KD, T + 2], F32R, offset=x_at)
            ffn_phase(nc, sems, "f1", x, x1, w_t, bias, gate_t, ics, ocs, ident, X)
            conv_phase(nc, sems, conv_w, conv_b, conv_out, X, (wq, wk, wv, wo), x_room)
            attention_phase(nc, sems, conv_out, x1, x2, x_room, wp, bq, bk, bv, bo, bp, ident)
        ffn_phase(nc, sems, "f2", x2, out, w_t, bias, gate_t, ics, ocs, ident, None)


def kernel(**inputs):
    import numpy as _np
    import concourse.bacc as _bacc
    from concourse import mybir as _mybir
    from concourse.bass_utils import run_bass_kernel_spmd as _run

    a = {n.removeprefix("L0_"): _np.asarray(v) for n, v in inputs.items()}

    def chunked(w, n):
        return w.reshape(n, P, -1).transpose(1, 0, 2).reshape(P, -1)

    def columns(b):
        return b.reshape(-1, P).T

    laid = {
        "x": a["attn_inputs"].reshape(T, D),
        "conv_w": a["attn_conv_w"].reshape(TAPS, 2, KQ, P, NCH, P).transpose(4, 1, 3, 0, 2, 5).reshape(NCH, 2, P, TAPS, KQ * P),
        "conv_b": columns(a["attn_conv_b"]),
        "wq": chunked(a["attn_wq"], WC), "bq": columns(a["attn_bq"]),
        "wk": chunked(a["attn_wk"], WC), "bk": columns(a["attn_bk"]),
        "wv": chunked(a["attn_wv"], WC), "bv": columns(a["attn_bv"]),
        "wo": chunked(a["attn_wo"].reshape(HE, W), KH), "bo": columns(a["attn_bo"]),
        "wp": chunked(a["attn_proj_w"], WC), "bp": a["attn_proj_b"],
        "w_t": a["ffn_weight"].T, "bias": a["ffn_bias"], "gate_t": a["ffn_gate_w"].T,
        "ics": a["ffn_in_channel_scale"], "ocs": a["ffn_out_channel_scale"],
    }
    nc = _bacc.Bacc("TRN2", target_bir_lowering=False, num_devices=1)
    arrays, args = {}, []
    for name, value in laid.items():
        value = _np.ascontiguousarray(value)
        arrays[f"in_{name}_dram"] = value
        args.append(nc.dram_tensor(f"in_{name}_dram", value.shape, _mybir.dt.from_np(value.dtype), kind="ExternalInput").ap())
    args.append(nc.dram_tensor("out_0_dram", (T, D), _mybir.dt.float32, kind="ExternalOutput").ap())
    macaron_kernel(nc, *args)
    r = _run(nc, [arrays], core_ids=[0])
    return r.results[0]["out_0_dram"].reshape(1, T, D)
```
